# Optimizing a Trainium2 kernel written in Bass

```python
import numpy as np
import jax
import jax.numpy as jnp

def _softmax(x, axis=-1):
    return jax.nn.softmax(x, axis=axis)

def _gelu(x):
    return jax.nn.gelu(x, approximate=True)

def _silu(x):
    return jax.nn.silu(x)

def _sigmoid(x):
    return jax.nn.sigmoid(x)

def _layernorm(x, axis=-1, eps=1e-05):
    m = jnp.mean(x, axis=axis, keepdims=True)
    v = jnp.var(x, axis=axis, keepdims=True)
    return (x - m) / jnp.sqrt(v + eps)

def _scatter_add(tgt, idx, src, axis=0):
    return tgt.at[idx].add(src)

def _segment_sum(src, seg, n):
    return jax.ops.segment_sum(src, seg, n)
kernel_name = 'mk_decoder_preln_d1_seqx_r8_8c12b9'

def setup_inputs(seed: int=0):
    np.random.seed(seed)
    _w = jnp.asarray

    def _rec_inputs():
        import jax
        import jax.numpy as jnp
        _rk = jax.random.key(seed)
        x = 7.22e-05 + 1 * jax.random.normal(jax.random.fold_in(_rk, 1), (8, 128, 512), jnp.float32)
        _lenS = 128 - jax.random.randint(jax.random.fold_in(_rk, 7), (8,), 0, max(1, 128 // 4) + 1, jnp.int32)
        _lenS2 = 128 - jax.random.randint(jax.random.fold_in(_rk, 8), (8,), 0, max(1, 128 // 4) + 1, jnp.int32)
        _ctx_4096P = jax.random.normal(jax.random.fold_in(_rk, 11), (8, 16, 512), jnp.float32)
        _ctx_4096c = jax.random.dirichlet(jax.random.fold_in(_rk, 511), 0.3 * jnp.ones((16,), jnp.float32), (8, 128))
        _ctx_4096t = jnp.einsum('bsk,bkd->bsd', _ctx_4096c, _ctx_4096P)
        _ctx_4096t = _ctx_4096t * jax.lax.rsqrt(jnp.mean(jnp.square(_ctx_4096t)) + 1e-12) * 0.953939
        ctx_4096 = 4.13588e-05 + 0.999923 * (_ctx_4096t + 0.3 * jax.random.normal(jax.random.fold_in(_rk, 611), (8, 128, 512), jnp.float32))
        _validS = jnp.arange(128)[None, :] < _lenS[:, None]
        _validS2 = jnp.arange(128)[None, :] < _lenS2[:, None]
        _causal = jnp.tril(jnp.ones((128, 128), dtype=bool))
        mask_BxSxS2_bk0 = jnp.logical_not(jnp.broadcast_to(_validS2[:, None, :], (8, 128, 128)))
        return (x, ctx_4096, mask_BxSxS2_bk0)
    x, ctx_4096, mask_BxSxS2_bk0 = _rec_inputs()

    def _L0_attn_setup():
        import math
        import jax, jax.numpy as jnp
        import numpy as np
        B, T, E = (2, 256, 512)
        H, HKV = (32, 8)
        DH = E // H
        G = H // HKV
        ROPE_THETA = 500000.0
        ROPE_FACTOR = 32.0
        HI_FREQ_FACTOR = 4.0
        LO_FREQ_FACTOR = 1.0
        ORIG_CTX = 1024

        def _rope_cos_sin(t_len):
            inv_freq = 1.0 / ROPE_THETA ** (jnp.arange(0, DH, 2, dtype=jnp.float32) / DH)
            wavelen = 2.0 * math.pi / inv_freq
            cut_lo = ORIG_CTX / HI_FREQ_FACTOR
            cut_hi = ORIG_CTX / LO_FREQ_FACTOR
            inv_freq = jnp.where(wavelen > cut_hi, inv_freq / ROPE_FACTOR, inv_freq)
            smooth = (ORIG_CTX / wavelen - LO_FREQ_FACTOR) / (HI_FREQ_FACTOR - LO_FREQ_FACTOR)
            smoothed = (1.0 - smooth) * inv_freq / ROPE_FACTOR + smooth * inv_freq
            is_medium = ~(wavelen < cut_hi) & ~(wavelen > cut_lo)
            inv_freq = jnp.where(is_medium, smoothed, inv_freq)
            pos = jnp.arange(t_len, dtype=jnp.float32)
            freqs = pos[:, None] * inv_freq[None, :]
            emb = jnp.concatenate([freqs, freqs], axis=-1)
            return (jnp.cos(emb), jnp.sin(emb))

        def _rotate_half(x):
            x1, x2 = jnp.split(x, 2, axis=-1)
            return jnp.concatenate([-x2, x1], axis=-1)
        key = jax.random.key(seed)
        kx, kq, kk, kv, ko = jax.random.split(key, 5)
        w = lambda k, shape: jax.random.normal(k, shape, jnp.float32) * 0.02
        return {'x': jax.random.normal(kx, (B, T, E), jnp.float32), 'Wq': w(kq, (E, E)), 'Wk': w(kk, (HKV * DH, E)), 'Wv': w(kv, (HKV * DH, E)), 'Wo': w(ko, (E, E))}
    _L0_attn_all = _L0_attn_setup()
    _L0_attn_in = {k: v for k, v in _L0_attn_all.items() if k in ('Wq', 'Wk', 'Wv', 'Wo')}
    del _L0_attn_all

    def _L0_xattn_setup():
        import jax, jax.numpy as jnp
        import numpy as np
        B, LQ, LK, D, H, DH = (2, 128, 128, 512, 32, 128)
        EPS = 1e-05

        def _rmsnorm(x, weight):
            var = jnp.mean(jnp.square(x), axis=-1, keepdims=True)
            return x * jax.lax.rsqrt(var + EPS) * weight
        key = jax.random.key(seed)
        ks = jax.random.split(key, 8)
        scale = 0.02
        return {'hidden_states': jax.random.normal(ks[0], (B, LQ, D), jnp.float32), 'key_value_states': jax.random.normal(ks[1], (B, LK, D), jnp.float32), 'attention_mask': jax.random.randint(ks[2], (B, LQ, LK), 0, 2) > 0, 'position_bias': jax.random.normal(ks[3], (H, LQ, LK), jnp.float32), 'ln_weight': jnp.ones((D,), jnp.float32), 'w_q': jax.random.normal(ks[4], (H * DH, D), jnp.float32) * scale, 'w_k': jax.random.normal(ks[5], (H * DH, D), jnp.float32) * scale, 'w_v': jax.random.normal(ks[6], (H * DH, D), jnp.float32) * scale, 'w_out': jax.random.normal(ks[7], (D, H * DH), jnp.float32) * scale}
    _L0_xattn_all = _L0_xattn_setup()
    _L0_xattn_in = {k: v for k, v in _L0_xattn_all.items() if k in ('position_bias', 'ln_weight', 'w_q', 'w_k', 'w_v', 'w_out')}
    del _L0_xattn_all

    def _L0_ffn_setup():
        import jax, jax.numpy as jnp
        import numpy as np
        LORA_RANK = 16
        LORA_ALPHA = 16
        LORA_SCALE = LORA_ALPHA / LORA_RANK
        key = jax.random.key(seed)
        k1, k2, k3, k4, k5 = jax.random.split(key, 5)
        B, S, D_IN, D_OUT, N_LORA, R = (8, 256, 512, 512, 3, LORA_RANK)
        std = 1.0 / np.sqrt(D_IN)
        x = jax.random.normal(k1, (B, S, D_IN), dtype=jnp.float32)
        weight = jax.random.truncated_normal(k2, -3.0, 3.0, (D_OUT, D_IN), dtype=jnp.float32) * std
        bias = jax.random.normal(k3, (D_OUT,), dtype=jnp.float32) * 0.01
        lora_A = jax.random.normal(k4, (N_LORA, R, D_IN), dtype=jnp.float32) * std
        lora_B = jax.random.normal(k5, (N_LORA, D_OUT, R), dtype=jnp.float32) * 0.02
        lora_start_indices = jnp.arange(4, dtype=jnp.int64) * 2
        return {'x': x, 'weight': weight, 'bias': bias, 'lora_A': lora_A, 'lora_B': lora_B, 'lora_start_indices': lora_start_indices}
    _L0_ffn_all = _L0_ffn_setup()
    _L0_ffn_in = {k: v for k, v in _L0_ffn_all.items() if k in ('weight', 'bias', 'lora_A', 'lora_B', 'lora_start_indices')}
    del _L0_ffn_all
    return {'x': x, 'ctx_4096': ctx_4096, 'mask_BxSxS2_bk0': mask_BxSxS2_bk0, 'L0_attn_Wq': _L0_attn_in['Wq'], 'L0_attn_Wk': _L0_attn_in['Wk'], 'L0_attn_Wv': _L0_attn_in['Wv'], 'L0_attn_Wo': _L0_attn_in['Wo'], 'L0_xattn_position_bias': _L0_xattn_in['position_bias'], 'L0_xattn_ln_weight': _L0_xattn_in['ln_weight'], 'L0_xattn_w_q': _L0_xattn_in['w_q'], 'L0_xattn_w_k': _L0_xattn_in['w_k'], 'L0_xattn_w_v': _L0_xattn_in['w_v'], 'L0_xattn_w_out': _L0_xattn_in['w_out'], 'L0_ffn_weight': _L0_ffn_in['weight'], 'L0_ffn_bias': _L0_ffn_in['bias'], 'L0_ffn_lora_A': _L0_ffn_in['lora_A'], 'L0_ffn_lora_B': _L0_ffn_in['lora_B'], 'L0_ffn_lora_start_indices': _L0_ffn_in['lora_start_indices']}

def reference(x, ctx_4096, mask_BxSxS2_bk0, L0_attn_Wq, L0_attn_Wk, L0_attn_Wv, L0_attn_Wo, L0_xattn_position_bias, L0_xattn_ln_weight, L0_xattn_w_q, L0_xattn_w_k, L0_xattn_w_v, L0_xattn_w_out, L0_ffn_weight, L0_ffn_bias, L0_ffn_lora_A, L0_ffn_lora_B, L0_ffn_lora_start_indices):
    import jax
    import jax.numpy as jnp

    def _L0_attn_ref(x, Wq, Wk, Wv, Wo):
        import math
        import jax, jax.numpy as jnp
        import numpy as np
        B, T, E = (2, 256, 512)
        H, HKV = (32, 8)
        DH = E // H
        G = H // HKV
        ROPE_THETA = 500000.0
        ROPE_FACTOR = 32.0
        HI_FREQ_FACTOR = 4.0
        LO_FREQ_FACTOR = 1.0
        ORIG_CTX = 1024

        def _rope_cos_sin(t_len):
            inv_freq = 1.0 / ROPE_THETA ** (jnp.arange(0, DH, 2, dtype=jnp.float32) / DH)
            wavelen = 2.0 * math.pi / inv_freq
            cut_lo = ORIG_CTX / HI_FREQ_FACTOR
            cut_hi = ORIG_CTX / LO_FREQ_FACTOR
            inv_freq = jnp.where(wavelen > cut_hi, inv_freq / ROPE_FACTOR, inv_freq)
            smooth = (ORIG_CTX / wavelen - LO_FREQ_FACTOR) / (HI_FREQ_FACTOR - LO_FREQ_FACTOR)
            smoothed = (1.0 - smooth) * inv_freq / ROPE_FACTOR + smooth * inv_freq
            is_medium = ~(wavelen < cut_hi) & ~(wavelen > cut_lo)
            inv_freq = jnp.where(is_medium, smoothed, inv_freq)
            pos = jnp.arange(t_len, dtype=jnp.float32)
            freqs = pos[:, None] * inv_freq[None, :]
            emb = jnp.concatenate([freqs, freqs], axis=-1)
            return (jnp.cos(emb), jnp.sin(emb))

        def _rotate_half(x):
            x1, x2 = jnp.split(x, 2, axis=-1)
            return jnp.concatenate([-x2, x1], axis=-1)
        b, t, _ = x.shape
        q = (x @ Wq.T).reshape(b, t, H, DH).transpose(0, 2, 1, 3)
        k = (x @ Wk.T).reshape(b, t, HKV, DH).transpose(0, 2, 1, 3)
        v = (x @ Wv.T).reshape(b, t, HKV, DH).transpose(0, 2, 1, 3)
        cos, sin = _rope_cos_sin(t)
        cos = cos.astype(x.dtype)[None, None]
        sin = sin.astype(x.dtype)[None, None]
        q = q * cos + _rotate_half(q) * sin
        k = k * cos + _rotate_half(k) * sin
        qg = q.reshape(b, HKV, G, t, DH)
        scores = jnp.einsum('bhgtd,bhkd->bhgtk', qg.astype(jnp.float32), k.astype(jnp.float32)) / math.sqrt(DH)
        causal = jnp.tril(jnp.ones((t, t), dtype=bool))
        scores = jnp.where(causal[None, None, None], scores, jnp.finfo(jnp.float32).min)
        attn = jax.nn.softmax(scores, axis=-1).astype(x.dtype)
        ctx = jnp.einsum('bhgtk,bhkd->bhgtd', attn, v)
        out = ctx.reshape(b, H, t, DH).transpose(0, 2, 1, 3).reshape(b, t, E)
        return out @ Wo.T

    def _L0_xattn_ref(hidden_states, key_value_states, attention_mask, position_bias, ln_weight, w_q, w_k, w_v, w_out):
        import jax, jax.numpy as jnp
        import numpy as np
        B, LQ, LK, D, H, DH = (2, 128, 128, 512, 32, 128)
        EPS = 1e-05

        def _rmsnorm(x, weight):
            var = jnp.mean(jnp.square(x), axis=-1, keepdims=True)
            return x * jax.lax.rsqrt(var + EPS) * weight
        x = _rmsnorm(hidden_states, ln_weight)
        b, lq, _ = x.shape
        lk = key_value_states.shape[1]
        h_q = (x @ w_q.T).reshape(b, lq, H, DH)
        h_k = (key_value_states @ w_k.T).reshape(b, lk, H, DH)
        h_v = (key_value_states @ w_v.T).reshape(b, lk, H, DH)
        score = jnp.einsum('bqhd,bkhd->bhqk', h_q, h_k)
        score = score + position_bias[None]
        m = attention_mask[:, None]
        score = jnp.where(m, score, -jnp.inf)
        score = jax.nn.softmax(score, axis=-1)
        score = jnp.where(m, score, 0.0)
        attn = jnp.einsum('bhqk,bkhd->bqhd', score, h_v).reshape(b, lq, H * DH)
        out = attn @ w_out.T
        return hidden_states + out

    def _L0_ffn_ref(x, weight, bias, lora_A, lora_B, lora_start_indices):
        import jax, jax.numpy as jnp
        import numpy as np
        LORA_RANK = 16
        LORA_ALPHA = 16
        LORA_SCALE = LORA_ALPHA / LORA_RANK
        y = jnp.einsum('bsd,od->bso', x, weight) + bias
        B = x.shape[0]
        seg = jnp.searchsorted(lora_start_indices, jnp.arange(B), side='right') - 1
        adapter_idx = jnp.clip(seg - 1, 0, lora_A.shape[0] - 1)
        A = lora_A[adapter_idx]
        Bw = lora_B[adapter_idx]
        lo = jnp.einsum('bsr,bor->bso', jnp.einsum('bsd,brd->bsr', x, A), Bw) * LORA_SCALE
        use_lora = (seg > 0)[:, None, None]
        return y + jnp.where(use_lora, lo, jnp.zeros((), dtype=y.dtype))
    x = x + _L0_attn_ref(_layernorm(x, axis=-1), L0_attn_Wq, L0_attn_Wk, L0_attn_Wv, L0_attn_Wo)
    x = x + _L0_xattn_ref(_layernorm(x, axis=-1), ctx_4096, mask_BxSxS2_bk0, L0_xattn_position_bias, L0_xattn_ln_weight, L0_xattn_w_q, L0_xattn_w_k, L0_xattn_w_v, L0_xattn_w_out)
    x = x + _L0_ffn_ref(_layernorm(x, axis=-1), L0_ffn_weight, L0_ffn_bias, L0_ffn_lora_A, L0_ffn_lora_B, L0_ffn_lora_start_indices)
    return x

_drawn_inputs = setup_inputs


def setup_inputs(seed=0):
    import zlib

    import numpy as np

    out = dict(_drawn_inputs(seed))
    spreads = {'L0_xattn_ln_weight': (1.0, 0.2)}
    factors = {'L0_attn_Wq': 7.163, 'L0_attn_Wk': 6.342, 'L0_ffn_bias': 8.0}
    for name, (base, spread) in spreads.items():
        noise = np.random.default_rng([zlib.crc32(name.encode()), seed]).standard_normal(out[name].shape)
        drawn = base * np.exp(spread * noise) if base else spread * noise
        out[name] = jnp.asarray(drawn.astype(out[name].dtype))
    for name, factor in factors.items():
        out[name] = (out[name] * factor).astype(out[name].dtype)
    return out
```

```python
from contextlib import ExitStack

import concourse.bass as bass
from concourse import mybir

F32 = mybir.dt.float32
F32R = mybir.dt.float32r
BF16 = mybir.dt.bfloat16
U8 = mybir.dt.uint8
I32 = mybir.dt.int32
ALU = mybir.AluOpType
ACT = mybir.ActivationFunctionType
AX = mybir.AxisListType

P = 128
NB = 8
D = 512
EC = D // P
EPS = 1e-5
MASKED = -1e30
SH, SKV, SD = 32, 8, 16
GR = SH // SKV
QUADS = SKV // 4
GROUPS = 4 * QUADS
SSCALE = SD ** -0.5
XH_ = 32
PAIRS = XH_ // 2
STEPS = PAIRS * NB
HALF = NB // 2
LOOP = 2 * NB
HEAD = LOOP - HALF
ROUNDS = (STEPS - LOOP) // LOOP
TAIL = STEPS - HEAD - ROUNDS * LOOP
PART = 1024
RANK = 48
PG_SQ, PG_SKVO, PG_CTX, PG_X0 = 0, 1, 2, 3
PG_FFN = PG_X0 + PAIRS
NPAGES = PG_FFN + 1
C_TABQ, C_COSK, C_SINK, C_SEL, C_CAUSAL, C_IDENT = 0, 128, 256, 384, 384 + 1024, 384 + 1152
C_BATCH, C_ROWS = C_IDENT + 128, C_IDENT + 136
NCONST = C_IDENT + 137


def build(nc, x, pages, mask, posbias, lnw, ffn_bias, lora_b, starts, consts, out):
    with ExitStack() as ctx:
        def sb(name, shape, dt=F32, scope=ctx):
            return scope.enter_context(nc.sbuf_tensor(name, shape, dt))

        def sem(name):
            return ctx.enter_context(nc.semaphore(name))

        bank = [ctx.enter_context(nc.psum_tensor(f"bank{i}", [P, 512], F32)) for i in range(8)]

        acc = sb("acc", [P, NB * D])
        XTH = sb("XTH", [P, EC * NB * P], F32R)
        XTL = sb("XTL", [P, EC * NB * P], F32R)
        CTH = sb("CTH", [P, EC * NB * P], F32R)
        CTL = sb("CTL", [P, EC * NB * P], F32R)
        raw = [sb(f"raw{i}", [P, PART]) for i in range(4)]
        WH = [sb(f"WH{i}", [P, 4 * PART], F32R) for i in range(2)]
        WL = [sb(f"WL{i}", [P, 4 * PART], F32R) for i in range(2)]
        ident = sb("ident", [P, P])
        mv = sb("mv", [P, NB * 2])
        st6 = sb("st6", [P, NB * 6])
        veps = sb("veps", [P, NB])
        rstd = sb("rstd", [P, NB])
        rms = sb("rms", [P, NB])
        mhalf = sb("mhalf", [P, NB])
        row = [sb(f"row{i}", [P, D]) for i in range(2)]

        s_raw = [sem(f"raw_loaded{i}") for i in range(4)]
        raw_free = [sem(f"raw_split{i}") for i in range(4)]
        s_x = [sem(f"x_loaded{b}") for b in range(NB)]
        s_const = sem("consts_loaded")
        s_mask = sem("mask_loaded")
        s_lnw, s_small = sem("lnw_loaded"), sem("small_loaded")
        s_pb = [sem(f"posbias_loaded{i}") for i in range(2)]
        hi_done = [sem(f"page_high{i}") for i in range(4)]
        st_done, mv_done, ve_done, rstd_done = sem("stats"), sem("moments"), sem("var_eps"), sem("rstd")
        rms_v, rms_ready = sem("rms_var"), sem("rms_ready")
        half_set = sem("half_set")
        xn_done, p_x, x_hi, x_lo = sem("xn_done"), sem("x_transposed"), sem("x_high"), sem("x_low")
        p_q, q_rope, p_kv, k_part, kv_ev = sem("q_mm"), sem("q_rope"), sem("kv_mm"), sem("k_part"), sem("kv_evac")
        p_ks, ks_ev = sem("kspread_mm"), sem("kspread_evac")
        p_s, v_stt, v_max, a_exp, p_t, pt_ev, p_pv = (sem(n) for n in (
            "s_scores", "s_masked", "s_max", "s_exp", "s_transposed", "s_pt_evac", "s_pv"))
        o_rec, o_norm, p_ot, ot_hi, ot_lo, p_w, w_acc = (sem(n) for n in (
            "o_recip", "o_norm", "o_transposed", "o_high", "o_low", "s_out_mm", "s_out_acc"))
        hid, xq, hadd, b_x, b_hi, b_lo = (sem(n) for n in (
            "hidden", "xq", "hidden_added", "b_transposed", "b_high", "b_low"))
        va1, valid_done, madd_done = sem("mask_f"), sem("valid_done"), sem("mask_add")
        qk_mm, v_mm, qk_hi, v_hi, qk_lo, v_lo = (sem(n) for n in (
            "qk_mm", "v_mm", "qk_high", "v_high", "qk_low", "v_low"))
        bm_done = sem("bias_mask")
        c_s, c_add, c_max, c_exp, c_rec, c_norm, c_t, c_thi, c_tlo = (sem(n) for n in (
            "c_scores", "c_added", "c_max", "c_exp", "c_recip", "c_norm", "c_transposed", "c_thigh", "c_tlow"))
        c_pv, c_ohi, c_olo, c_out, c_acc = (sem(n) for n in ("c_pv", "c_ohigh", "c_olow", "c_out", "c_acc"))
        f_n, f_x, f_hi, f_lo, f_a, f_am, f_ahi, f_alo, f_y, f_o = (sem(n) for n in (
            "f_norm", "f_transposed", "f_high", "f_low", "f_lora_mm", "f_lora_masked", "f_lora_high",
            "f_lora_low", "f_mm", "f_sum"))
        f_out = [sem(f"f_stored{i}") for i in range(2)]
        f_bias, f_bhi, f_blo, co = sem("f_bias"), sem("f_loraB_high"), sem("f_loraB_low"), sem("coef")
        co_done = sem("coef_done")

        def at_least(eng, s, n):
            if isinstance(n, int) and n <= 0:
                return
            eng.wait_ge(s, n)

        def page_slot(g):
            if g == PG_SQ:
                return XTH, XTL
            if g == PG_SKVO:
                return WH[1], WL[1]
            if g == PG_CTX:
                return CTH, CTL
            return WH[(g - PG_X0) % 2], WL[(g - PG_X0) % 2]

        def page_piece(t, q):
            j, slot = q % NB, (q // NB) % 2
            if j == 2 and (not isinstance(t, int) or t > NB):
                return (t - j) // NB + PG_X0 + 1, 3, 1 - slot
            if j in (4, 5, 6) and (not isinstance(t, int) or t < STEPS - NB):
                return (t - j) // NB + PG_X0 + 2, j - 4, slot
            return None

        def part(t, i):
            return t[:, i * PART:(i + 1) * PART]

        def bcast(ap, n):
            return ap.unsqueeze(1).to_broadcast([P, n, ap.shape[1]])

        def split3(nc, out_ap, aH, aL, bH, bL, start, stop):
            nc.tensor.matmul(out_ap, aH, bH, start=start, stop=False)
            nc.tensor.matmul(out_ap, aH, bL, start=False, stop=False)
            return nc.tensor.matmul(out_ap, aL, bH, start=False, stop=stop)

        sa = ExitStack()
        cst = sb("cst", [P, NCONST], scope=sa)
        tabq, cosk, sink = cst[:, C_TABQ:C_TABQ + P], cst[:, C_COSK:C_COSK + P], cst[:, C_SINK:C_SINK + P]
        causal = cst[:, C_CAUSAL:C_CAUSAL + P]
        xTH, xTL = sb("xTH", [P, D], F32R, sa), sb("xTL", [P, D], F32R, sa)
        qT = [[sb(f"qT{p}{q}", [P, D], scope=sa) for q in range(QUADS)] for p in range(2)]
        kS = [[sb(f"kS{p}{q}", [P, D], scope=sa) for q in range(QUADS)] for p in range(2)]
        vS = [sb(f"vS{p}", [P, P], scope=sa) for p in range(2)]
        kr = [sb(f"kr{i}", [P, P], scope=sa) for i in range(3)]
        sP = [sb(f"sP{i}", [P, D], scope=sa) for i in range(4)]
        smax = [sb(f"smax{i}", [P, 4], scope=sa) for i in range(4)]
        ssum = [sb(f"ssum{p}", [P, SH], scope=sa) for p in range(2)]
        srec = sb("srec", [P, SH], scope=sa)
        sPT = [sb(f"sPT{i}", [P, D], scope=sa) for i in range(2)]
        so = row[1]
        soTH, soTL = WH[1][:, PART + D:2 * PART], WL[1][:, PART + D:2 * PART]
        sa.close()
        ca = ExitStack()
        QH, QL, KH, KL = ([[sb(f"{n}{f}{h}", [P, D], F32R, ca) for h in range(2)] for f in range(2)]
                          for n in ("QH", "QL", "KH", "KL"))
        VH, VL = ([[sb(f"{n}{f}{k}", [P, 2 * P], F32R, ca) for k in range(HALF)] for f in range(2)]
                  for n in ("VH", "VL"))
        mask8 = sb("mask8", [P, NB * P], U8, ca)
        madd = sb("madd", [P, NB * P], BF16, ca)
        valid = sb("valid", [P, NB], scope=ca)
        pb = [sb(f"pb{i}", [P, 2 * P], scope=ca) for i in range(2)]
        cP, bm = ([row[j][:, i * 2 * P:(i + 1) * 2 * P] for i in range(2)] for j in range(2))
        cmax = [sb(f"cmax{i}", [P, 2], scope=ca) for i in range(2)]
        csum = [sb(f"csum{i}", [P, 2], scope=ca) for i in range(2)]
        crec = [sb(f"crec{i}", [P, 2], scope=ca) for i in range(2)]
        cTH, cTL = sb("cTH", [P, 2 * P], F32R, ca), sb("cTL", [P, 2 * P], F32R, ca)
        oTH, oTL = sb("oTH", [P, 2 * P], F32R, ca), sb("oTL", [P, 2 * P], F32R, ca)
        ca.close()
        lw = ExitStack()
        lnw_b = sb("lnw_b", [P, D], scope=lw)
        hidden = [sb(f"hidden{i}", [P, D], scope=lw) for i in range(2)]
        lw.close()
        fl = ExitStack()
        bias_b = sb("bias_b", [P, D], scope=fl)
        coefc = sb("coefc", [RANK, 9], scope=fl)
        st_i = sb("st_i", [RANK, 4], I32, fl)
        st_f = sb("st_f", [RANK, 4], scope=fl)
        cnt = sb("cnt", [RANK, 5 * NB], scope=fl)
        coef = sb("coef", [RANK, NB], scope=fl)
        lb = sb("lb", [RANK, D], scope=fl)
        lbH, lbL = sb("lbH", [RANK, D], F32R, fl), sb("lbL", [RANK, D], F32R, fl)
        la = [sb(f"la{i}", [RANK, P], scope=fl) for i in range(2)]
        laH = [sb(f"laH{i}", [RANK, P], F32R, fl) for i in range(2)]
        laL = [sb(f"laL{i}", [RANK, P], F32R, fl) for i in range(2)]
        yo = [sb(f"yo{i}", [P, D], scope=fl) for i in range(2)]
        fl.close()

        bS, bPT, bO, bPJ, bW = bank[0:4], bank[4], bank[5], bank[6], bank[7]
        bQK, bV, bSC, bT, bPV, bOUT = bank[0:6]

        block = ctx.enter_context(nc.Block())

        @block.sync
        def _(sp):
            sp.dma_start(acc[:, 0:D], x[0]).then_inc(s_x[0], 16)
            sp.dma_start(cst[:], consts).then_inc(s_const, 16)
            sp.dma_start(ident[:], consts[:, C_IDENT:C_IDENT + P]).then_inc(s_const, 16)
            for g in range(NPAGES):
                for i in range(4):
                    at_least(sp, raw_free[i], g)
                    sp.dma_start(raw[i][:], pages[g, i]).then_inc(s_raw[i], 16)
                if g == 0:
                    for b in range(1, NB):
                        sp.dma_start(acc[:, b * D:(b + 1) * D], x[b]).then_inc(s_x[b], 16)
                if g == PG_X0:
                    sp.wait_ge(w_acc, NB)
                    sp.wait_ge(p_w, NB)
                    sp.dma_start(lnw_b[:], lnw.partition_broadcast(P)).then_inc(s_lnw, 16)
                    sp.dma_start(mask8[:].rearrange("p (b k) -> p b k", b=NB),
                                 mask.rearrange("b q k -> q b k")).then_inc(s_mask, 16)
                    for p in range(2):
                        sp.dma_start(pb[p][:].rearrange("p (h k) -> p h k", h=2),
                                     posbias[2 * p:2 * p + 2].rearrange("h q k -> q h k")).then_inc(s_pb[p], 16)
                if g > PG_X0 + 1 and g - PG_X0 < PAIRS:
                    p = g - PG_X0
                    sp.wait_ge(bm_done, NB * (p - 1))
                    sp.dma_start(pb[p % 2][:].rearrange("p (h k) -> p h k", h=2),
                                 posbias[2 * p:2 * p + 2].rearrange("h q k -> q h k")).then_inc(s_pb[p % 2], 16)
            sp.wait_ge(c_out, STEPS)
            sp.dma_start(bias_b[:], ffn_bias.partition_broadcast(P)).then_inc(s_small, 16)
            sp.dma_start(st_i[:], starts.partition_broadcast(RANK)).then_inc(s_small, 16)
            sp.dma_start(coefc[:], consts[0:RANK, C_BATCH:C_BATCH + 9]).then_inc(s_small, 16)
            sp.dma_start(lb[:], lora_b).then_inc(s_small, 16)
            for b in range(NB):
                sp.wait_ge(f_o, b + 1)
                sp.dma_start(out[b], yo[b % 2][:]).then_inc(f_out[b % 2], 16)
            for i in range(2):
                sp.wait_ge(f_out[i], 16 * NB // 2)

        @block.tensor
        def _(pe):
            def transposes(src, dst, done):
                for e in range(EC):
                    i = nc.tensor.transpose(dst[:, e * P:(e + 1) * P], src[:, e * P:(e + 1) * P], ident[:])
                i.then_inc(done, 1)

            def s_x_t(n):
                at_least(pe, ks_ev, 2 * n)
                pe.wait_ge(xn_done, n + 1)
                transposes(row[0], bPJ, p_x)

            def s_q(n, quad):
                for j in range(4):
                    c = 4 * quad + j
                    for e in range(EC):
                        w = slice(e * PART + c * P, e * PART + (c + 1) * P)
                        i = split3(nc, bPJ[:, j * P:(j + 1) * P], XTH[:, w], XTL[:, w],
                                   xTH[:, e * P:(e + 1) * P], xTL[:, e * P:(e + 1) * P],
                                   e == 0, e == EC - 1)
                i.then_inc(p_q, 1)

            def s_kv(n):
                pe.wait_ge(q_rope, 2 * n + 2)
                for o, off in ((0, 0), (1, 512)):
                    for e in range(EC):
                        w = slice(off + e * P, off + (e + 1) * P)
                        split3(nc, bPJ[:, o * P:(o + 1) * P], WH[1][:, w], WL[1][:, w],
                               xTH[:, e * P:(e + 1) * P], xTL[:, e * P:(e + 1) * P], e == 0, e == EC - 1)
                for e in range(EC):
                    w = slice(PART + e * P, PART + (e + 1) * P)
                    i = split3(nc, bPJ[:, 2 * P:3 * P], xTH[:, e * P:(e + 1) * P], xTL[:, e * P:(e + 1) * P],
                               WH[1][:, w], WL[1][:, w], e == 0, e == EC - 1)
                i.then_inc(p_kv, 1)

            def s_kspread(n, quad):
                if quad == 0:
                    pe.wait_ge(kv_ev, n + 1)
                else:
                    pe.wait_ge(ks_ev, 2 * n + 1)
                for j in range(4):
                    c = 4 * quad + j
                    i = nc.tensor.matmul(bPJ[:, j * P:(j + 1) * P], cst[:, C_SEL + c * P:C_SEL + (c + 1) * P],
                                         kr[2][:], start=True, stop=True)
                i.then_inc(p_ks, 1)

            def s_scores(b, g, par):
                h, quad = g % 4, g // 4
                if h == 0:
                    pe.wait_ge(q_rope, 2 * b + 1 + quad)
                    pe.wait_ge(ks_ev, 2 * b + 1 + quad)
                at_least(pe, v_stt, GROUPS * b + g - 3)
                r = slice(32 * h, 32 * h + 32)
                for j in range(4):
                    i = nc.tensor.matmul(bS[h][:, j * P:(j + 1) * P], qT[par][quad][r, j * P:(j + 1) * P],
                                         kS[par][quad][r, j * P:(j + 1) * P], start=True, stop=True)
                i.then_inc(p_s, 1)

            def s_probs_t(b, g):
                G = GROUPS * b + g
                pe.wait_ge(a_exp, G + 1)
                at_least(pe, pt_ev, G)
                for j in range(4):
                    i = nc.tensor.transpose(bPT[:, j * P:(j + 1) * P], sP[g % 4][:, j * P:(j + 1) * P], ident[:])
                i.then_inc(p_t, 1)

            def s_values(b, g, par):
                G = GROUPS * b + g
                pe.wait_ge(pt_ev, G + 1)
                if g == 0:
                    pe.wait_ge(kv_ev, b + 1)
                    at_least(pe, o_norm, b)
                for j in range(4):
                    kv = 4 * (g // 4) + j
                    head = GR * kv + g % 4
                    i = nc.tensor.matmul(bO[:, head * SD:(head + 1) * SD], sPT[g % 2][:, j * P:(j + 1) * P],
                                         vS[par][:, kv * SD:(kv + 1) * SD], start=True, stop=True)
                i.then_inc(p_pv, 1)

            def s_o_t(b):
                pe.wait_ge(o_norm, b + 1)
                transposes(so, bPJ, p_ot)

            def s_out(b):
                pe.wait_ge(ot_lo, b + 1)
                at_least(pe, w_acc, b)
                for e in range(EC):
                    w = slice(2 * PART + e * D, 2 * PART + (e + 1) * D)
                    i = split3(nc, bW[:], soTH[:, e * P:(e + 1) * P], soTL[:, e * P:(e + 1) * P],
                               WH[1][:, w], WL[1][:, w], e == 0, e == EC - 1)
                i.then_inc(p_w, 1)

            def s_batch(b, par, project=True, first=False):
                n = b + 1
                s_scores(b, 0, par)
                s_scores(b, 1, par)
                for g in range(GROUPS):
                    if g + 2 < GROUPS:
                        s_scores(b, g + 2, par)
                    s_probs_t(b, g)
                    if g:
                        s_values(b, g - 1, par)
                    if project and g == 0:
                        s_x_t(n)
                    if project and g == 1:
                        pe.wait_ge(x_lo, n + 1)
                        s_q(n, 0)
                    if not first and g == 2:
                        pe.wait_ge(q_rope, 2 * n + 1) if project else pe.wait_ge(ks_ev, 2 * n)
                        s_o_t(b - 1)
                    if project and g == 3:
                        pe.wait_ge(q_rope, 2 * n + 1) if first else pe.wait_ge(ot_lo, b)
                        s_q(n, 1)
                    if project and g == 4:
                        s_kv(n)
                    if not first and g == 5:
                        s_out(b - 1)
                    if project and g == 6:
                        s_kspread(n, 0)
                    if project and g == 7:
                        s_kspread(n, 1)
                s_values(b, GROUPS - 1, par)

            pe.wait_ge(s_const, 32)
            s_x_t(0)
            pe.wait_ge(x_lo, 1)
            for i in range(4):
                pe.wait_ge(raw_free[i], PG_SQ + 1)
            s_q(0, 0)
            pe.wait_ge(q_rope, 1)
            s_q(0, 1)
            for i in range(4):
                pe.wait_ge(raw_free[i], PG_SKVO + 1)
            s_kv(0)
            s_kspread(0, 0)
            s_kspread(0, 1)
            s_batch(0, 0, first=True)
            with pe.Fori(0, (NB - 2) // 2) as r:
                for par in (1, 0):
                    s_batch(2 * r + (1 if par else 2), par)
            s_batch(NB - 1, 1, project=False)
            pe.wait_ge(ot_lo, NB - 1)
            s_o_t(NB - 1)
            s_out(NB - 1)

            for b in range(NB):
                pe.wait_ge(xq, b + 1)
                at_least(pe, b_lo, b - 1)
                transposes(row[b % 2], bank[6 + b % 2], b_x)

            def c_project_qk(n, q):
                k, f, slot = q % 4, (q // 4) % 2, (q // 8) % 2
                head, keys = k // 2, k % 2
                if q % 8 == 0:
                    pe.wait_ge(raw_free[0], PG_X0 + 1 + n // 8)
                if q % 8 == 1:
                    pe.wait_ge(raw_free[1], PG_X0 + 1 + n // 8)
                at_least(pe, qk_lo, n)
                XH, XL = (CTH, CTL) if keys else (XTH, XTL)
                for e in range(EC):
                    w = slice(keys * PART + e * 2 * P + head * P, keys * PART + e * 2 * P + (head + 1) * P)
                    m = slice(e * NB * P + f * HALF * P, e * NB * P + (f + 1) * HALF * P)
                    i = split3(nc, bQK[:], WH[slot][:, w], WL[slot][:, w], XH[:, m], XL[:, m],
                               e == 0, e == EC - 1)
                i.then_inc(qk_mm, 1)

            def c_project_v(n, q):
                b, slot = q % 8, (q // 8) % 2
                if q % 8 == 0:
                    pe.wait_ge(raw_free[2], PG_X0 + 1 + n // 8)
                at_least(pe, v_lo, n)
                for e in range(EC):
                    m = slice(e * NB * P + b * P, e * NB * P + (b + 1) * P)
                    w = slice(2 * PART + e * 2 * P, 2 * PART + (e + 1) * 2 * P)
                    i = split3(nc, bV[:, 0:2 * P], CTH[:, m], CTL[:, m], WH[slot][:, w], WL[slot][:, w],
                               e == 0, e == EC - 1)
                i.then_inc(v_mm, 1)

            def c_scores(t, q):
                f, k = (q // 4) % 2, q % 4
                if k == 0:
                    pe.wait_ge(qk_lo, t + HALF)
                at_least(pe, c_add, t)
                c = slice(k * P, (k + 1) * P)
                for h in range(2):
                    i = split3(nc, bSC[:, h * P:(h + 1) * P], QH[f][h][:, c], QL[f][h][:, c],
                               KH[f][h][:, c], KL[f][h][:, c], True, True)
                i.then_inc(c_s, 1)

            def c_probs_t(t, q):
                pe.wait_ge(c_norm, t + 1)
                at_least(pe, c_tlo, t)
                for h in range(2):
                    i = nc.tensor.transpose(bT[:, h * P:(h + 1) * P], cP[q % 2][:, h * P:(h + 1) * P], ident[:])
                i.then_inc(c_t, 1)

            def c_values(t, q):
                f, k = (q // 4) % 2, q % 4
                pe.wait_ge(c_tlo, t + 1)
                pe.wait_ge(v_lo, t + 1)
                at_least(pe, c_olo, t)
                for h in range(2):
                    c = slice(h * P, (h + 1) * P)
                    i = split3(nc, bPV[:, c], VH[f][k][:, c], VL[f][k][:, c], cTH[:, c], cTL[:, c], True, True)
                i.then_inc(c_pv, 1)

            def c_output(t, q):
                slot = (q // 8) % 2
                if q % 8 == 0:
                    pe.wait_ge(raw_free[3], PG_X0 + 1 + t // 8)
                pe.wait_ge(c_olo, t + 1)
                at_least(pe, c_acc, t)
                for h in range(2):
                    c, w = slice(h * P, (h + 1) * P), slice(3 * PART + h * D, 3 * PART + (h + 1) * D)
                    i = split3(nc, bOUT[:], oTH[:, c], oTL[:, c], WH[slot][:, w], WL[slot][:, w],
                               h == 0, h == 1)
                i.then_inc(c_out, 1)

            def c_step(t, q):
                c_scores(t, q)
                if not isinstance(t, int) or t >= 1:
                    c_probs_t(t - 1, (q - 1) % LOOP)
                if not isinstance(t, int) or t >= 2:
                    c_output(t - 2, (q - 2) % LOOP)
                ahead = not isinstance(t, int) or t + HALF < STEPS
                if ahead:
                    c_project_qk(t + HALF, (q + HALF) % LOOP)
                if not isinstance(t, int) or t >= 1:
                    c_values(t - 1, (q - 1) % LOOP)
                if ahead:
                    c_project_v(t + HALF, (q + HALF) % LOOP)

            for i in range(4):
                pe.wait_ge(raw_free[i], PG_CTX + 1)
            pe.wait_ge(b_lo, NB)
            for n in range(HALF):
                c_project_qk(n, n)
                c_project_v(n, n)
            for t in range(HEAD):
                c_step(t, t)
            with pe.Fori(0, ROUNDS) as r:
                for q in range(LOOP):
                    c_step(r * LOOP + (HEAD + q), (HEAD + q) % LOOP)
            for t in range(STEPS - TAIL, STEPS):
                c_step(t, t % LOOP)
            last = STEPS - 1
            c_probs_t(last, last % LOOP)
            c_output(last - 1, (last - 1) % LOOP)
            c_values(last, last % LOOP)
            c_output(last, last % LOOP)

            W, L = WH[(PG_FFN - PG_X0) % 2], WL[(PG_FFN - PG_X0) % 2]
            for b in range(NB):
                pe.wait_ge(f_n, b + 1)
                if b >= 1:
                    pe.wait_ge(f_lo, b)
                transposes(row[b % 2], bank[0], f_x)
                pe.wait_ge(f_lo, b + 1)
                if b >= 1:
                    pe.wait_ge(f_am, b)
                for e in range(EC):
                    m = slice(e * NB * P + b * P, e * NB * P + (b + 1) * P)
                    w = slice(2 * PART + e * RANK, 2 * PART + (e + 1) * RANK)
                    i = split3(nc, bank[1][0:RANK, 0:P], W[:, w], L[:, w], XTH[:, m], XTL[:, m],
                               e == 0, e == EC - 1)
                i.then_inc(f_a, 1)
                y = bank[2 + b % 2]
                at_least(pe, f_o, b - 1)
                for e in range(EC):
                    m = slice(e * NB * P + b * P, e * NB * P + (b + 1) * P)
                    w = slice(e * D, (e + 1) * D)
                    split3(nc, y[:], XTH[:, m], XTL[:, m], W[:, w], L[:, w], e == 0, False)
                pe.wait_ge(f_alo, b + 1)
                pe.wait_ge(f_blo, 1)
                split3(nc, y[:], laH[b % 2][:], laL[b % 2][:], lbH[:], lbL[:], False, True).then_inc(f_y, 1)

        @block.scalar
        def _(act):
            def copy(dst, src):
                return nc.scalar.activation(dst, src, ACT.Copy)

            def high(g):
                H, _ = page_slot(g)
                for i in range(4):
                    act.wait_ge(s_raw[i], 16 * (g + 1))
                    copy(part(H, i), raw[i][:]).then_inc(hi_done[i], 1)

            def high_piece(t, q):
                piece = page_piece(t, q)
                if not piece:
                    return
                g, i, slot = piece
                if i == 3:
                    act.wait_ge(c_out, t - 2)
                else:
                    act.wait_ge(qk_mm, t - i + 4)
                    act.wait_ge(v_mm, t - i + 4)
                act.wait_ge(s_raw[i], 16 * (g + 1))
                copy(part(WH[slot], i), raw[i][:]).then_inc(hi_done[i], 1)

            def s_x_hi(n):
                act.wait_ge(p_x, n + 1)
                copy(xTH[:], bPJ[:]).then_inc(x_hi, 1)

            def s_kspread_evac(n, par, quad):
                act.wait_ge(p_ks, 2 * n + 1 + quad)
                copy(kS[par][quad][:], bPJ[:]).then_inc(ks_ev, 1)

            def s_exp(b, g, par):
                act.wait_ge(v_max, GROUPS * b + g + 1)
                for j in range(4):
                    head = GR * (4 * (g // 4) + j) + g % 4
                    c = sP[g % 4][:, j * P:(j + 1) * P]
                    i = nc.scalar.activation(c, c, ACT.Exp, bias=smax[g % 4][:, j:j + 1],
                                             accum_out=ssum[par][:, head:head + 1])
                i.then_inc(a_exp, 1)

            def s_o_hi(b):
                act.wait_ge(p_ot, b + 1)
                copy(soTH, bPJ[:]).then_inc(ot_hi, 1)

            def s_batch(b, par, project=True, first=False):
                n = b + 1
                s_exp(b, 0, par)
                for g in range(GROUPS):
                    if g + 1 < GROUPS:
                        s_exp(b, g + 1, par)
                    if project and g == 0:
                        s_x_hi(n)
                    if not first and g == 2:
                        s_o_hi(b - 1)
                    if project and g >= 6:
                        s_kspread_evac(n, 1 - par, g - 6)

            high(PG_SQ)
            s_x_hi(0)
            high(PG_SKVO)
            s_kspread_evac(0, 0, 0)
            s_kspread_evac(0, 0, 1)
            s_batch(0, 0, first=True)
            high(PG_CTX)
            with act.Fori(0, (NB - 2) // 2) as r:
                for par in (1, 0):
                    s_batch(2 * r + (1 if par else 2), par)
            high(PG_X0)
            s_batch(NB - 1, 1, project=False)
            s_o_hi(NB - 1)

            for b in range(NB):
                act.wait_ge(b_x, b + 1)
                copy(XTH[:].rearrange("p (e t) -> p e t", e=EC)[:, :, b * P:(b + 1) * P],
                     bank[6 + b % 2][:].rearrange("p (e t) -> p e t", e=EC)).then_inc(b_hi, 1)

            def c_qk_hi(n, q):
                k, f = q % 4, (q // 4) % 2
                act.wait_ge(qk_mm, n + 1)
                copy((KH if k % 2 else QH)[f][k // 2][:], bQK[:]).then_inc(qk_hi, 1)

            def c_v_hi(n, q):
                act.wait_ge(v_mm, n + 1)
                copy(VH[(q // 4) % 2][q % 4][:], bV[:, 0:2 * P]).then_inc(v_hi, 1)

            def c_t_hi(t, q):
                act.wait_ge(c_t, t + 1)
                at_least(act, c_pv, t)
                copy(cTH[:], bT[:, 0:2 * P]).then_inc(c_thi, 1)

            def c_exps(t, q):
                act.wait_ge(c_max, t + 1)
                for h in range(2):
                    c = cP[q % 2][:, h * P:(h + 1) * P]
                    i = nc.scalar.activation(c, c, ACT.Exp, bias=cmax[q % 2][:, h:h + 1],
                                             accum_out=csum[q % 2][:, h:h + 1])
                i.then_inc(c_exp, 1)

            def c_o_hi(t, q):
                act.wait_ge(c_pv, t + 1)
                at_least(act, c_out, t)
                copy(oTH[:], bPV[:, 0:2 * P]).then_inc(c_ohi, 1)

            def c_step(t, q):
                if not isinstance(t, int) or t >= 1:
                    c_t_hi(t - 1, (q - 1) % LOOP)
                c_exps(t, q)
                ahead = not isinstance(t, int) or t + HALF < STEPS
                if ahead:
                    c_qk_hi(t + HALF, (q + HALF) % LOOP)
                if not isinstance(t, int) or t >= 1:
                    c_o_hi(t - 1, (q - 1) % LOOP)
                if ahead:
                    c_v_hi(t + HALF, (q + HALF) % LOOP)
                high_piece(t, q)

            act.wait_ge(xq, NB)
            act.wait_ge(hadd, NB)
            for n in range(HALF):
                c_qk_hi(n, n)
                c_v_hi(n, n)
            high(PG_X0 + 1)
            for t in range(HEAD):
                c_step(t, t)
            with act.Fori(0, ROUNDS) as r:
                for q in range(LOOP):
                    c_step(r * LOOP + (HEAD + q), (HEAD + q) % LOOP)
            for t in range(STEPS - TAIL, STEPS):
                c_step(t, t % LOOP)
            c_t_hi(STEPS - 1, (STEPS - 1) % LOOP)
            c_o_hi(STEPS - 1, (STEPS - 1) % LOOP)

            act.wait_ge(s_small, 16 * 4)
            copy(lbH[:], lb[:]).then_inc(f_bhi, 1)
            for b in range(NB):
                act.wait_ge(f_x, b + 1)
                copy(XTH[:].rearrange("p (e t) -> p e t", e=EC)[:, :, b * P:(b + 1) * P],
                     bank[0][:].rearrange("p (e t) -> p e t", e=EC)).then_inc(f_hi, 1)
                act.wait_ge(f_am, b + 1)
                at_least(act, f_y, b - 1)
                copy(laH[b % 2][:], la[b % 2][:]).then_inc(f_ahi, 1)

        @block.vector
        def _(dve):
            v = nc.vector

            def moments(k, b, ready=None, count=0):
                if ready is not None:
                    dve.wait_ge(ready, count)
                v.bn_stats(st6[:, 6 * b:6 * b + 6], acc[:, b * D:(b + 1) * D]).then_inc(st_done, 1)
                dve.wait_ge(st_done, NB * k + b + 1)
                v.bn_aggr(mv[:, 2 * b:2 * b + 2], st6[:, 6 * b:6 * b + 6]).then_inc(mv_done, 1)

            def var_eps(k):
                dve.wait_ge(mv_done, NB * (k + 1))
                v.tensor_scalar(veps[:], mv[:].rearrange("p (b s) -> p b s", s=2)[:, :, 1], EPS, None,
                                ALU.add).then_inc(ve_done, 1)

            def low(g):
                H, L = page_slot(g)
                for i in range(4):
                    dve.wait_ge(hi_done[i], g + 1)
                    v.tensor_tensor(part(L, i), raw[i][:], part(H, i).bitcast(F32), ALU.subtract)\
                     .then_inc(raw_free[i], 1)

            def s_xn(n):
                at_least(dve, p_x, n)
                v.tensor_scalar(row[0][:], acc[:, bass.ts(n, D)], mv[:, bass.ds(2 * n, 1)],
                                rstd[:, bass.ds(n, 1)], ALU.subtract, ALU.mult).then_inc(xn_done, 1)

            def s_x_lo(n):
                dve.wait_ge(x_hi, n + 1)
                v.tensor_tensor(xTL[:], bPJ[:], xTH[:].bitcast(F32), ALU.subtract).then_inc(x_lo, 1)

            def s_rope_q(n, par, quad):
                dve.wait_ge(p_q, 2 * n + 1 + quad)
                v.tensor_tensor(qT[par][quad][:].rearrange("p (c t) -> p c t", c=4),
                                bPJ[:].rearrange("p (c t) -> p c t", c=4), bcast(tabq, 4),
                                ALU.mult).then_inc(q_rope, 1)

            def s_kv_evac(n, par):
                dve.wait_ge(p_kv, n + 1)
                at_least(dve, p_ks, 2 * n)
                v.tensor_tensor(kr[0][:], bPJ[:, 0:P], cosk, ALU.mult).then_inc(k_part, 1)
                v.tensor_tensor(kr[1][:], bPJ[:, P:2 * P], sink, ALU.mult).then_inc(k_part, 1)
                v.tensor_copy(vS[par][:], bPJ[:, 2 * P:3 * P]).then_inc(k_part, 1)
                dve.wait_ge(k_part, 3 * n + 3)
                v.tensor_tensor(kr[2][:], kr[0][:], kr[1][:], ALU.add).then_inc(kv_ev, 1)

            def s_mask_max(b, g):
                G = GROUPS * b + g
                dve.wait_ge(p_s, G + 1)
                at_least(dve, p_t, G - 3)
                v.scalar_tensor_tensor(out=sP[g % 4][:].rearrange("p (c t) -> p c t", c=4),
                                       in0=bS[g % 4][:].rearrange("p (c t) -> p c t", c=4), scalar=SSCALE,
                                       in1=bcast(causal, 4), op0=ALU.mult, op1=ALU.add).then_inc(v_stt, 1)
                dve.wait_ge(v_stt, G + 1)
                v.tensor_reduce(smax[g % 4][:], sP[g % 4][:].rearrange("p (c t) -> p c t", c=4), AX.X,
                                ALU.max, negate=True).then_inc(v_max, 1)

            def s_probs_evac(b, g):
                G = GROUPS * b + g
                dve.wait_ge(p_t, G + 1)
                at_least(dve, p_pv, G - 1)
                v.tensor_copy(sPT[g % 2][:], bPT[:]).then_inc(pt_ev, 1)

            def s_o_norm(b, par):
                dve.wait_ge(a_exp, GROUPS * (b + 1))
                v.reciprocal(srec[:], ssum[par][:]).then_inc(o_rec, 1)
                dve.wait_ge(o_rec, b + 1)
                dve.wait_ge(p_pv, GROUPS * (b + 1))
                at_least(dve, p_ot, b)
                v.tensor_tensor(so[:].rearrange("p (h d) -> p h d", d=SD),
                                bO[:].rearrange("p (h d) -> p h d", d=SD),
                                srec[:].unsqueeze(2).to_broadcast([P, SH, SD]), ALU.mult).then_inc(o_norm, 1)

            def s_o_lo(b):
                dve.wait_ge(ot_hi, b + 1)
                v.tensor_tensor(soTL, bPJ[:], soTH.bitcast(F32), ALU.subtract).then_inc(ot_lo, 1)

            def s_acc(b):
                dve.wait_ge(p_w, b + 1)
                v.tensor_tensor(acc[:, bass.ts(b, D)], bW[:], acc[:, bass.ts(b, D)], ALU.add)\
                 .then_inc(w_acc, 1)

            def s_batch(b, par, project=True, first=False):
                n = b + 1
                if project:
                    s_xn(n)
                s_mask_max(b, 0)
                s_mask_max(b, 1)
                if not first:
                    s_o_norm(b - 1, 1 - par)
                for g in range(GROUPS):
                    if g + 2 < GROUPS:
                        s_mask_max(b, g + 2)
                    s_probs_evac(b, g)
                    if project and g == 0:
                        s_x_lo(n)
                    if project and g == 1:
                        s_rope_q(n, 1 - par, 0)
                    if not first and g == 2:
                        s_o_lo(b - 1)
                    if project and g == 3:
                        s_rope_q(n, 1 - par, 1)
                    if project and g == 4:
                        s_kv_evac(n, 1 - par)
                    if not first and g == 5:
                        s_acc(b - 1)

            for b in range(NB):
                moments(0, b, s_x[b], 16)
            var_eps(0)
            dve.wait_ge(s_const, 32)
            dve.wait_ge(rstd_done, 1)
            s_xn(0)
            low(PG_SQ)
            s_x_lo(0)
            s_rope_q(0, 0, 0)
            s_rope_q(0, 0, 1)
            low(PG_SKVO)
            s_kv_evac(0, 0)
            s_batch(0, 0, first=True)
            with dve.Fori(0, (NB - 2) // 2) as r:
                for par in (1, 0):
                    s_batch(2 * r + (1 if par else 2), par)
            s_batch(NB - 1, 1, project=False)
            s_o_norm(NB - 1, 1)
            s_o_lo(NB - 1)
            s_acc(NB - 1)

            dve.wait_ge(w_acc, NB)
            for b in range(NB):
                moments(1, b)
            var_eps(1)
            dve.wait_ge(rstd_done, 2)
            v.tensor_tensor(rms[:], rstd[:], rstd[:], ALU.mult).then_inc(rms_v, 1)
            dve.wait_ge(rms_v, 1)
            v.tensor_tensor(rms[:], rms[:], mv[:].rearrange("p (b s) -> p b s", s=2)[:, :, 1], ALU.mult)\
             .then_inc(rms_v, 1)
            dve.wait_ge(rms_v, 2)
            v.tensor_scalar(rms[:], rms[:], EPS, None, ALU.add).then_inc(rms_v, 1)
            dve.wait_ge(s_lnw, 16)
            dve.wait_ge(rms_ready, 1)

            def x_norm(b):
                a = acc[:, b * D:(b + 1) * D]
                at_least(dve, hadd, b - 1)
                v.tensor_scalar(hidden[b % 2][:], a, mv[:, 2 * b:2 * b + 1], rstd[:, b:b + 1],
                                ALU.subtract, ALU.mult).then_inc(hid, 1)
                dve.wait_ge(hid, b + 1)
                at_least(dve, b_x, b - 1)
                v.scalar_tensor_tensor(out=row[b % 2][:], in0=hidden[b % 2][:], scalar=rms[:, b:b + 1],
                                       in1=lnw_b[:], op0=ALU.mult, op1=ALU.mult).then_inc(xq, 1)
                v.tensor_tensor(a, a, hidden[b % 2][:], ALU.add).then_inc(hadd, 1)

            def x_lo_part(b):
                dve.wait_ge(b_hi, b + 1)
                c = XTL[:].rearrange("p (e t) -> p e t", e=EC)[:, :, b * P:(b + 1) * P]
                h = XTH[:].bitcast(F32).rearrange("p (e t) -> p e t", e=EC)[:, :, b * P:(b + 1) * P]
                v.tensor_tensor(c, bank[6 + b % 2][:].rearrange("p (e t) -> p e t", e=EC), h,
                                ALU.subtract).then_inc(b_lo, 1)

            x_norm(0)
            for b in range(1, NB):
                x_norm(b)
                x_lo_part(b - 1)
            x_lo_part(NB - 1)
            dve.wait_ge(s_mask, 16)
            dve.wait_ge(hadd, NB)
            v.tensor_reduce(valid[:], mask8[:].rearrange("p (b k) -> p b k", b=NB), AX.X, ALU.max)\
             .then_inc(valid_done, 1)
            v.tensor_scalar(madd[:], mask8[:], 1.0, -MASKED, ALU.subtract, ALU.mult).then_inc(madd_done, 1)
            dve.wait_ge(valid_done, 1)

            def c_qk_lo(n, q):
                k, f = q % 4, (q // 4) % 2
                H, L = (KH, KL) if k % 2 else (QH, QL)
                dve.wait_ge(qk_hi, n + 1)
                v.tensor_tensor(L[f][k // 2][:], bQK[:], H[f][k // 2][:].bitcast(F32), ALU.subtract)\
                 .then_inc(qk_lo, 1)

            def c_v_lo(n, q):
                f, k = (q // 4) % 2, q % 4
                dve.wait_ge(v_hi, n + 1)
                v.tensor_tensor(VL[f][k][:], bV[:, 0:2 * P], VH[f][k][:].bitcast(F32), ALU.subtract)\
                 .then_inc(v_lo, 1)

            def c_add_max(t, q):
                dve.wait_ge(c_s, t + 1)
                dve.wait_ge(bm_done, t + 1)
                at_least(dve, c_t, t - 1)
                v.tensor_tensor(cP[q % 2], bSC[:, 0:2 * P], bm[q % 2], ALU.add).then_inc(c_add, 1)
                dve.wait_ge(c_add, t + 1)
                v.tensor_reduce(cmax[q % 2][:], cP[q % 2].rearrange("p (h k) -> p h k", h=2), AX.X,
                                ALU.max, negate=True).then_inc(c_max, 1)

            def c_t_lo(t, q):
                dve.wait_ge(c_thi, t + 1)
                v.tensor_tensor(cTL[:], bT[:, 0:2 * P], cTH[:].bitcast(F32), ALU.subtract).then_inc(c_tlo, 1)

            def c_normalise(t, q):
                b = q % NB
                dve.wait_ge(c_exp, t + 1)
                v.reciprocal(crec[q % 2][:], csum[q % 2][:]).then_inc(c_rec, 1)
                dve.wait_ge(c_rec, t + 1)
                for h in range(2):
                    c = cP[q % 2][:, h * P:(h + 1) * P]
                    i = v.tensor_scalar(c, c, crec[q % 2][:, h:h + 1], valid[:, b:b + 1], ALU.mult, ALU.mult)
                i.then_inc(c_norm, 1)

            def c_accumulate(t, q):
                b = q % NB
                dve.wait_ge(c_out, t + 1)
                at_least(dve, c_acc, t - NB + 1)
                a = acc[:, b * D:(b + 1) * D]
                v.tensor_tensor(a, bOUT[:], a, ALU.add).then_inc(c_acc, 1)

            def c_o_lo(t, q):
                dve.wait_ge(c_ohi, t + 1)
                v.tensor_tensor(oTL[:], bPV[:, 0:2 * P], oTH[:].bitcast(F32), ALU.subtract).then_inc(c_olo, 1)

            def c_step(t, q):
                c_add_max(t, q)
                if not isinstance(t, int) or t >= 1:
                    c_t_lo(t - 1, (q - 1) % LOOP)
                c_normalise(t, q)
                if not isinstance(t, int) or t >= 2:
                    c_accumulate(t - 2, (q - 2) % LOOP)
                ahead = not isinstance(t, int) or t + HALF < STEPS
                if ahead:
                    c_qk_lo(t + HALF, (q + HALF) % LOOP)
                if not isinstance(t, int) or t >= 1:
                    c_o_lo(t - 1, (q - 1) % LOOP)
                if ahead:
                    c_v_lo(t + HALF, (q + HALF) % LOOP)

            for n in range(HALF):
                c_qk_lo(n, n)
                c_v_lo(n, n)
            for t in range(HEAD):
                c_step(t, t)
            with dve.Fori(0, ROUNDS) as r:
                for q in range(LOOP):
                    c_step(r * LOOP + (HEAD + q), (HEAD + q) % LOOP)
            for t in range(STEPS - TAIL, STEPS):
                c_step(t, t % LOOP)
            last = STEPS - 1
            c_t_lo(last, last % LOOP)
            c_accumulate(last - 1, (last - 1) % LOOP)
            c_o_lo(last, last % LOOP)
            c_accumulate(last, last % LOOP)

            dve.wait_ge(c_acc, STEPS)
            for b in range(NB):
                moments(2, b)
            var_eps(2)
            dve.wait_ge(s_small, 16 * 4)
            v.tensor_copy(st_f[:], st_i[:]).then_inc(co, 1)
            dve.wait_ge(co, 1)
            for i in range(4):
                v.tensor_scalar(cnt[:, i * NB:(i + 1) * NB], coefc[:, 0:NB], st_f[:, i:i + 1], None, ALU.is_ge)\
                 .then_inc(co, 1)
            dve.wait_ge(co, 5)
            v.tensor_reduce(cnt[:, 4 * NB:5 * NB], cnt[:, 0:4 * NB].rearrange("p (i b) -> p b i", i=4), AX.X,
                            ALU.add).then_inc(co, 1)
            dve.wait_ge(co, 6)
            v.tensor_scalar(coef[:], cnt[:, 4 * NB:5 * NB], coefc[:, NB:NB + 1], None, ALU.is_equal)\
             .then_inc(co_done, 1)
            dve.wait_ge(f_bhi, 1)
            v.tensor_tensor(lbL[:], lb[:], lbH[:].bitcast(F32), ALU.subtract).then_inc(f_blo, 1)
            dve.wait_ge(rstd_done, 3)
            dve.wait_ge(co_done, 1)

            def f_norm(b):
                at_least(dve, f_x, b - 1)
                v.tensor_scalar(row[b % 2][:], acc[:, b * D:(b + 1) * D], mv[:, 2 * b:2 * b + 1],
                                rstd[:, b:b + 1], ALU.subtract, ALU.mult).then_inc(f_n, 1)

            def f_sum(b):
                dve.wait_ge(f_y, b + 1)
                dve.wait_ge(f_bias, b + 1)
                at_least(dve, f_out[b % 2], 16 * (b // 2))
                v.tensor_tensor(yo[b % 2][:], bank[2 + b % 2][:], acc[:, b * D:(b + 1) * D], ALU.add)\
                 .then_inc(f_o, 1)

            f_norm(0)
            for b in range(NB):
                if b + 1 < NB:
                    f_norm(b + 1)
                dve.wait_ge(f_hi, b + 1)
                c = XTL[:].rearrange("p (e t) -> p e t", e=EC)[:, :, b * P:(b + 1) * P]
                h = XTH[:].bitcast(F32).rearrange("p (e t) -> p e t", e=EC)[:, :, b * P:(b + 1) * P]
                v.tensor_tensor(c, bank[0][:].rearrange("p (e t) -> p e t", e=EC), h, ALU.subtract)\
                 .then_inc(f_lo, 1)
                dve.wait_ge(f_a, b + 1)
                at_least(dve, f_alo, b - 1)
                v.tensor_scalar(la[b % 2][:], bank[1][0:RANK, 0:P], coef[:, b:b + 1], None, ALU.mult)\
                 .then_inc(f_am, 1)
                dve.wait_ge(f_ahi, b + 1)
                v.tensor_tensor(laL[b % 2][:], la[b % 2][:], laH[b % 2][:].bitcast(F32), ALU.subtract)\
                 .then_inc(f_alo, 1)
                if b:
                    f_sum(b - 1)
            f_sum(NB - 1)

        @block.gpsimd
        def _(pool):
            g_ = nc.gpsimd

            def low(g, i, slot=None):
                H, L = (WH[slot], WL[slot]) if slot is not None else page_slot(g)
                pool.wait_ge(hi_done[i], g + 1)
                g_.tensor_tensor(part(L, i), raw[i][:], part(H, i).bitcast(F32), ALU.subtract)\
                  .then_inc(raw_free[i], 1)

            g_.memset(mhalf[:], -0.5).then_inc(half_set, 1)
            pool.wait_ge(half_set, 1)
            pool.wait_ge(ve_done, 1)
            g_.tensor_tensor(rstd[:], veps[:], mhalf[:], ALU.pow).then_inc(rstd_done, 1)
            for i in range(4):
                low(PG_CTX, i)
            for i in range(4):
                low(PG_X0, i)
            pool.wait_ge(ve_done, 2)
            pool.wait_ge(xn_done, NB)
            g_.tensor_tensor(rstd[:], veps[:], mhalf[:], ALU.pow).then_inc(rstd_done, 1)
            pool.wait_ge(rms_v, 3)
            g_.tensor_tensor(rms[:], rms[:], mhalf[:], ALU.pow).then_inc(rms_ready, 1)

            def bias_mask(t, q):
                p, b = (q // NB) % 2, q % NB
                if b == 0:
                    pool.wait_ge(s_pb[p], 16 * (t // LOOP + 1))
                at_least(pool, c_add, t - 1)
                g_.tensor_tensor(bm[q % 2].rearrange("p (h k) -> p h k", h=2),
                                 pb[p][:].rearrange("p (h k) -> p h k", h=2),
                                 bcast(madd[:, b * P:(b + 1) * P], 2), ALU.add).then_inc(bm_done, 1)

            def c_step(t, q):
                if not isinstance(t, int) or t + 1 < STEPS:
                    bias_mask(t + 1, (q + 1) % LOOP)
                piece = page_piece(t, q)
                if piece:
                    low(*piece)

            pool.wait_ge(madd_done, 1)
            pool.wait_ge(b_x, NB)
            bias_mask(0, 0)
            for i in range(4):
                low(PG_X0 + 1, i)
            for t in range(HEAD):
                c_step(t, t)
            with pool.Fori(0, ROUNDS) as r:
                for q in range(LOOP):
                    c_step(r * LOOP + (HEAD + q), (HEAD + q) % LOOP)
            for t in range(STEPS - TAIL, STEPS):
                c_step(t, t % LOOP)

            pool.wait_ge(ve_done, 3)
            g_.tensor_tensor(rstd[:], veps[:], mhalf[:], ALU.pow).then_inc(rstd_done, 1)
            pool.wait_ge(s_small, 16 * 4)
            pool.wait_ge(c_acc, STEPS)
            for b in range(NB):
                a = acc[:, b * D:(b + 1) * D]
                pool.wait_ge(f_n, b + 1)
                g_.tensor_tensor(a, a, bias_b[:], ALU.add).then_inc(f_bias, 1)


def rope_tables(n):
    import numpy as np
    f = np.float32
    inv = (f(1.0) / f(500000.0) ** (np.arange(0, SD, 2, dtype=f) / f(SD))).astype(f)
    wavelen = (f(2.0 * np.pi) / inv).astype(f)
    low, high = 1024 / 4.0, 1024 / 1.0
    scaled = np.where(wavelen > high, inv / f(32.0), inv).astype(f)
    smooth = ((f(1024) / wavelen - f(1.0)) / f(3.0)).astype(f)
    smoothed = ((f(1.0) - smooth) * scaled / f(32.0) + smooth * scaled).astype(f)
    medium = ~(wavelen < high) & ~(wavelen > low)
    scaled = np.where(medium, smoothed, scaled).astype(f)
    freqs = np.arange(n, dtype=f)[:, None] * scaled[None, :]
    emb = np.concatenate([freqs, freqs], axis=-1).astype(f)
    return np.cos(emb).astype(f), np.sin(emb).astype(f)


def shape_constants():
    import numpy as np
    c = np.zeros((P, NCONST), np.float32)
    cos, sin = rope_tables(P)
    sign = np.where(np.arange(SD) < SD // 2, -1.0, 1.0).astype(np.float32)
    rot = (sin * sign).T
    c[:, C_TABQ:C_TABQ + P] = np.tile(np.concatenate([cos.T, rot]), (4, 1))
    c[:, C_COSK:C_COSK + P] = np.tile(cos.T, (SKV, 1))
    c[:, C_SINK:C_SINK + P] = np.tile(rot, (SKV, 1))
    for kv in range(SKV):
        for r in range(P):
            c[kv * SD + r % SD, C_SEL + kv * P + r] = 1.0
    c[:, C_CAUSAL:C_CAUSAL + P] = np.where(np.tril(np.ones((P, P), bool)), 0.0, MASKED)
    c[:, C_IDENT:C_IDENT + P] = np.eye(P)
    c[:, C_BATCH:C_BATCH + NB] = np.arange(NB)[None, :]
    c[:RANK, C_ROWS] = 2 + np.arange(RANK) // 16
    return c


def weight_pages(ctx, Wq, Wk, Wv, Wo, w_q, w_k, w_v, w_out, ffn, lora_a):
    import numpy as np

    def on_partitions(wT):
        return wT.reshape(EC, P, -1).transpose(1, 0, 2)

    pages = np.zeros((NPAGES, 4, P, PART), np.float32)
    swapped = (np.arange(SD) + SD // 2) % SD
    rows = np.concatenate([h * SD + np.concatenate([np.arange(SD), swapped]) for h in range(SH)])
    pages[PG_SQ] = on_partitions(Wq[rows].T).transpose(1, 0, 2)
    krows = np.concatenate([h * SD + swapped for h in range(SKV)])
    pages[PG_SKVO, 0, :, :512] = on_partitions(Wk.T).reshape(P, -1)
    pages[PG_SKVO, 0, :, 512:] = on_partitions(Wk[krows].T).reshape(P, -1)
    pages[PG_SKVO, 1, :, :512] = on_partitions(Wv.T).reshape(P, -1)
    pages[PG_SKVO, 2:4] = on_partitions(Wo.T).reshape(P, 2, PART).transpose(1, 0, 2)
    pages[PG_CTX] = on_partitions(ctx.reshape(NB * P, D).T).transpose(1, 0, 2)
    for p in range(PAIRS):
        r = slice(2 * P * p, 2 * P * (p + 1))
        for i, w in enumerate((w_q, w_k, w_v)):
            pages[PG_X0 + p, i] = on_partitions(w[r].T).reshape(P, PART)
        pages[PG_X0 + p, 3] = w_out[:, r].T.reshape(2, P, D).transpose(1, 0, 2).reshape(P, PART)
    pages[PG_FFN, 0:2] = on_partitions(ffn.T).reshape(P, 2, PART).transpose(1, 0, 2)
    pages[PG_FFN, 2, :, :EC * RANK] = on_partitions(lora_a.reshape(RANK, D).T).reshape(P, -1)
    return pages


def kernel(**inputs):
    import numpy as np
    import concourse.bacc as bacc
    from concourse.bass_utils import run_bass_kernel_spmd as run

    a = {k: np.asarray(v) for k, v in inputs.items()}
    arrays = {
        "x": a["x"],
        "pages": weight_pages(a["ctx_4096"], a["L0_attn_Wq"], a["L0_attn_Wk"], a["L0_attn_Wv"], a["L0_attn_Wo"],
                              a["L0_xattn_w_q"], a["L0_xattn_w_k"], a["L0_xattn_w_v"], a["L0_xattn_w_out"],
                              a["L0_ffn_weight"], a["L0_ffn_lora_A"]),
        "mask": a["mask_BxSxS2_bk0"],
        "posbias": a["L0_xattn_position_bias"],
        "lnw": a["L0_xattn_ln_weight"],
        "ffn_bias": a["L0_ffn_bias"],
        "lora_b": a["L0_ffn_lora_B"].transpose(0, 2, 1).reshape(RANK, D),
        "starts": a["L0_ffn_lora_start_indices"],
        "consts": shape_constants(),
    }
    nc = bacc.Bacc("TRN2", target_bir_lowering=False, num_devices=1,
                   dynamic_dma_scratch_size=1024)
    arrays = {f"in_{k}": np.ascontiguousarray(v) for k, v in arrays.items()}
    args = [nc.dram_tensor(k, v.shape, mybir.dt.from_np(v.dtype), kind="ExternalInput").ap()
            for k, v in arrays.items()]
    out = nc.dram_tensor("out", (NB, P, D), F32, kind="ExternalOutput").ap()
    build(nc, *args, out)
    r = run(nc, [arrays], core_ids=[0])
    return r.results[0]["out"]
```

```python
from contextlib import ExitStack

import concourse.bass as bass
from concourse import mybir

F32 = mybir.dt.float32
F32R = mybir.dt.float32r
BF16 = mybir.dt.bfloat16
U8 = mybir.dt.uint8
I32 = mybir.dt.int32
ALU = mybir.AluOpType
ACT = mybir.ActivationFunctionType
AX = mybir.AxisListType

P = 128
NB = 8
D = 512
EC = D // P
EPS = 1e-5
MASKED = -1e30
SH, SKV, SD = 32, 8, 16
GR = SH // SKV
GROUPS = 8
SLOTS = GROUPS * NB
QP = 4
SSCALE = SD ** -0.5
XH_ = 32
PAIRS = XH_ // 2
STEPS = PAIRS * NB
HALF = NB // 2
LOOP = 2 * NB
HEAD = LOOP - HALF
ROUNDS = (STEPS - LOOP) // LOOP
TAIL = STEPS - HEAD - ROUNDS * LOOP
PART = 1024
RANK = 48
F_STAT = {STEPS - 4: (0, 1, 2), STEPS - 3: (3,), STEPS - 2: (4,), STEPS - 1: (5,)}
F_TURN = {STEPS - 4: (), STEPS - 3: (0, 1), STEPS - 2: (2, 3), STEPS - 1: (4,)}
PG_SQ, PG_SKVO, PG_CTX, PG_X0 = 0, 1, 2, 3
PG_FFN = PG_X0 + PAIRS
NPAGES = PG_FFN + 1

BESIDE = ("x0", "o", "x1", "k", "w", "q0", "q1", "v", "s0", "o", "s1", "q2", "w", "q3", "s2", "s3")
BESIDE_LAST = ("", "o", "n0", "n1", "w", "n2", "n3", "n4", "", "o", "n5", "", "w", "", "n6", "")
TAIL_PIECES = ("o", "w", "", "n")
FIRST = ("x0", "x1", "q0", "q1", "q2", "q3", "k", "v", "s0", "s1", "s2", "s3")


def beside(slot):
    pair = slot // (2 * GROUPS)
    last = pair == NB // 2 - 1
    name = (BESIDE_LAST if last else BESIDE)[slot % (2 * GROUPS)]
    if not name:
        return None
    if name in ("o", "w"):
        b = slot // GROUPS - 1
        return (name, b) if b >= 0 else None
    if name[0] == "n":
        return "n", int(name[1])
    return name[0], (pair + 1, int(name[1:] or 0))


C_TABQ, C_COSK, C_SINK, C_SEL, C_CAUSAL, C_IDENT = 0, 128, 256, 384, 384 + 1024, 384 + 1152
C_BATCH, C_ROWS = C_IDENT + 128, C_IDENT + 136
NCONST = C_IDENT + 137


def build(nc, x, pages, mask, posbias, lnw, ffn_bias, starts, consts, out):
    with ExitStack() as ctx:
        def sb(name, shape, dt=F32, scope=ctx):
            return scope.enter_context(nc.sbuf_tensor(name, shape, dt))

        def sem(name):
            return ctx.enter_context(nc.semaphore(name))

        bank = [ctx.enter_context(nc.psum_tensor(f"bank{i}", [P, 512], F32)) for i in range(8)]

        acc = sb("acc", [P, NB * D])
        XTH = sb("XTH", [P, EC * NB * P], F32R)
        XTL = sb("XTL", [P, EC * NB * P], F32R)
        CTH = sb("CTH", [P, EC * NB * P], F32R)
        CTL = sb("CTL", [P, EC * NB * P], F32R)
        raw = [sb(f"raw{i}", [P, PART]) for i in range(4)]
        WH = [sb(f"WH{i}", [P, 4 * PART], F32R) for i in range(2)]
        WL = [sb(f"WL{i}", [P, 4 * PART], F32R) for i in range(2)]
        ident = sb("ident", [P, P])
        mv, mv2, mv3 = (sb(f"mv{i}", [P, NB * 2]) for i in (1, 2, 3))
        st6 = sb("st6", [P, NB * 6])
        veps, veps2, veps3 = (sb(f"veps{i}", [P, NB]) for i in (1, 2, 3))
        rstd, rstd2, rstd3 = (sb(f"rstd{i}", [P, NB]) for i in (1, 2, 3))
        rms = sb("rms", [P, NB])
        mhalf = sb("mhalf", [P, 1])
        coefc = sb("coefc", [RANK, 9])
        st_i = sb("st_i", [RANK, 4], I32)
        st_f = sb("st_f", [RANK, 4])
        cnt = sb("cnt", [RANK, 5 * NB])
        coef = sb("coef", [RANK, NB])
        row = [sb(f"row{i}", [P, D]) for i in range(2)]

        s_raw = [sem(f"raw_loaded{i}") for i in range(4)]
        raw_free = [sem(f"raw_split{i}") for i in range(4)]
        s_x = [sem(f"x_loaded{b}") for b in range(NB)]
        s_const, s_ident = sem("consts_loaded"), sem("ident_loaded")
        s_mask = sem("mask_loaded")
        s_lnw, s_small = sem("lnw_loaded"), sem("small_loaded")
        s_pb = [sem(f"posbias_loaded{i}") for i in range(2)]
        hi_done = [sem(f"page_high{i}") for i in range(4)]
        st_done, mv_done, ve_done, rstd_done = sem("stats"), sem("moments"), sem("var_eps"), sem("rstd")
        ms_step, rms_ready, half_set = sem("mean_square"), sem("rms_ready"), sem("half_set")
        xn_done, p_x, x_hi, x_lo = sem("xn_done"), sem("x_transposed"), sem("x_high"), sem("x_low")
        p_q, q_rope, p_k, k_part, k_rope = sem("q_mm"), sem("q_rope"), sem("k_mm"), sem("k_part"), sem("k_rope")
        p_v, v_evac, p_ks, ks_ev = sem("v_mm_s"), sem("v_evac"), sem("kspread_mm"), sem("kspread_evac")
        p_s, v_stt, v_max, a_exp, p_t, pt_ev, p_pv = (sem(n) for n in (
            "s_scores", "s_masked", "s_max", "s_exp", "s_transposed", "s_pt_evac", "s_pv"))
        o_rec, o_norm, p_ot, ot_hi, ot_lo, p_w, w_acc = (sem(n) for n in (
            "o_recip", "o_norm", "o_transposed", "o_high", "o_low", "s_out_mm", "s_out_acc"))
        hid, xq, hadd, b_x, b_hi, b_lo = (sem(n) for n in (
            "hidden", "xq", "hidden_added", "b_transposed", "b_high", "b_low"))
        va1, valid_done, madd_done = sem("mask_f"), sem("valid_done"), sem("mask_add")
        qk_mm, v_mm, qk_hi, v_hi, qk_lo, v_lo = (sem(n) for n in (
            "qk_mm", "v_mm", "qk_high", "v_high", "qk_low", "v_low"))
        bm_done = sem("bias_mask")
        c_s, c_add, c_max, c_exp, c_rec, c_norm, c_t, c_thi, c_tlo = (sem(n) for n in (
            "c_scores", "c_added", "c_max", "c_exp", "c_recip", "c_norm", "c_transposed", "c_thigh", "c_tlow"))
        c_half, c_odiff = sem("c_half_added"), sem("c_odiff")
        c_pv, c_ohi, c_olo, c_out, c_acc = (sem(n) for n in ("c_pv", "c_ohigh", "c_olow", "c_out", "c_acc"))
        f_n, f_x, f_hi, f_lo, f_a, f_am, f_ahi, f_alo, f_y, f_o = (sem(n) for n in (
            "f_norm", "f_transposed", "f_high", "f_low", "f_lora_mm", "f_lora_masked", "f_lora_high",
            "f_lora_low", "f_mm", "f_sum"))
        f_out = [sem(f"f_stored{i}") for i in range(2)]
        f_bias, co = sem("f_bias"), sem("coef")
        co_done, s_bias = sem("coef_done"), sem("bias_loaded")

        def at_least(eng, s, n):
            if isinstance(n, int) and n <= 0:
                return
            eng.wait_ge(s, n)

        def page_slot(g):
            if g == PG_SQ:
                return XTH, XTL
            if g == PG_SKVO:
                return WH[1], WL[1]
            if g == PG_CTX:
                return CTH, CTL
            return WH[(g - PG_X0) % 2], WL[(g - PG_X0) % 2]

        def page_piece(t, q):
            j, slot = q % NB, (q // NB) % 2
            if j == 2 and (not isinstance(t, int) or t > NB):
                return (t - j) // NB + PG_X0 + 1, 3, 1 - slot
            if j in (4, 5, 6) and (not isinstance(t, int) or t < STEPS - NB):
                return (t - j) // NB + PG_X0 + 2, j - 4, slot
            return None

        def part(t, i):
            return t[:, i * PART:(i + 1) * PART]

        def bcast(ap, n):
            return ap.unsqueeze(1).to_broadcast([P, n, ap.shape[1]])

        def halves(ap, i):
            return ap.rearrange("p (n x t) -> p n x t", x=2, t=P)[:, :, i, :]

        def blocks(ap):
            return ap.rearrange("p (n t) -> p n t", t=P)

        def split3_wide(nc, out_ap, aH, aL, bHL):
            nc.tensor.matmul(out_ap, aH, bHL, start=True, stop=False)
            return nc.tensor.matmul(out_ap[:, 0:P], aL, bHL[:, 0:P], start=False, stop=True)

        def split3(nc, out_ap, aH, aL, bH, bL, start, stop):
            nc.tensor.matmul(out_ap, aH, bH, start=start, stop=False)
            nc.tensor.matmul(out_ap, aH, bL, start=False, stop=False)
            return nc.tensor.matmul(out_ap, aL, bH, start=False, stop=stop)

        sa = ExitStack()
        cst = sb("cst", [P, C_IDENT], scope=sa)
        tabq, cosk, sink = cst[:, C_TABQ:C_TABQ + P], cst[:, C_COSK:C_COSK + P], cst[:, C_SINK:C_SINK + P]
        causal = cst[:, C_CAUSAL:C_CAUSAL + P]
        qT = [[sb(f"qT{p}{q}", [P, D], scope=sa) for q in range(QP)] for p in range(2)]
        kS = [[sb(f"kS{p}{q}", [P, D], scope=sa) for q in range(QP)] for p in range(2)]
        vS = [sb(f"vS{p}", [P, 2 * P], scope=sa) for p in range(2)]
        kr = [sb(f"kr{i}", [P, 2 * P], scope=sa) for i in range(2)]
        sP = [sb(f"sP{i}", [P, D], scope=sa) for i in range(4)]
        smax = [sb(f"smax{i}", [P, 4], scope=sa) for i in range(4)]
        ssum = [sb(f"ssum{p}", [P, SH], scope=sa) for p in range(2)]
        srec = sb("srec", [P, SH], scope=sa)
        sPT = [sb(f"sPT{i}", [P, D], scope=sa) for i in range(2)]
        lnw_b = sb("lnw_b", [P, D], scope=sa)
        so = row[1]
        xTH, xTL = CTH, CTL
        soTH, soTL = WH[1][:, PART + D:2 * PART], WL[1][:, PART + D:2 * PART]
        sa.close()
        ca = ExitStack()
        QH, QL = ([[sb(f"{n}{f}{h}", [P, D], F32R, ca) for h in range(2)] for f in range(2)]
                  for n in ("QH", "QL"))
        KHL = [[sb(f"KHL{f}{h}", [P, 2 * D], F32R, ca) for h in range(2)] for f in range(2)]
        VH, VL = ([[sb(f"{n}{f}{k}", [P, 2 * P], F32R, ca) for k in range(HALF)] for f in range(2)]
                  for n in ("VH", "VL"))
        madd = sb("madd", [P, NB * P], BF16, ca)
        valid = sb("valid", [P, NB], scope=ca)
        pb = [sb(f"pb{i}", [P, 2 * P], scope=ca) for i in range(2)]
        cP, bm = ([row[j][:, i * 2 * P:(i + 1) * 2 * P] for i in range(2)] for j in range(2))
        cmax = [sb(f"cmax{i}", [P, 2], scope=ca) for i in range(2)]
        csum = [sb(f"csum{i}", [P, 2], scope=ca) for i in range(2)]
        crec = [sb(f"crec{i}", [P, 2], scope=ca) for i in range(2)]
        first = ExitStack()
        mask8 = sb("mask8", [P, NB * P], U8, first)
        first.close()
        cT = sb("cT", [P, 4 * P], F32R, ca)
        oD = sb("oD", [P, 2 * P], scope=ca)
        oTH, oTL = sb("oTH", [P, 2 * P], F32R, ca), sb("oTL", [P, 2 * P], F32R, ca)
        ca.close()
        frow = [raw[i][:, 0:D] for i in range(2)]
        yo = [raw[i][:, D:2 * D] for i in range(2)]
        bias_b = raw[2][:, 0:D]
        la = raw[3][0:RANK, :]
        fW, fL = WH[(PG_FFN - PG_X0) % 2], WL[(PG_FFN - PG_X0) % 2]
        lbH, lbL = (w[0:RANK, 3 * PART:3 * PART + D] for w in (fW, fL))
        laH, laL = (w[1 - (PG_FFN - PG_X0) % 2][0:RANK, 0:PART] for w in (WH, WL))

        bS, bPT, bO, bPJ, bW = bank[0:4], bank[4], bank[5], bank[6], bank[7]
        bQK, bV, bSC, bT, bPV, bOUT = bank[0:6]

        block = ctx.enter_context(nc.Block())

        @block.sync
        def _(sp):
            sp.dma_start(acc[:, 0:D], x[0]).then_inc(s_x[0], 16)
            sp.dma_start(acc[:, D:2 * D], x[1]).then_inc(s_x[1], 16)
            sp.dma_start(ident[:], consts[:, C_IDENT:C_IDENT + P]).then_inc(s_ident, 16)
            for g in range(NPAGES):
                for i in range(4):
                    at_least(sp, raw_free[i], g)
                    sp.dma_start(raw[i][:], pages[g, i]).then_inc(s_raw[i], 16)
                if g == 0:
                    sp.dma_start(cst[:], consts[:, 0:C_IDENT]).then_inc(s_const, 16)
                    for b in range(2, NB):
                        sp.dma_start(acc[:, b * D:(b + 1) * D], x[b]).then_inc(s_x[b], 16)
                    sp.dma_start(lnw_b[:], lnw.partition_broadcast(P)).then_inc(s_lnw, 16)
                    sp.dma_start(st_i[:], starts.partition_broadcast(RANK)).then_inc(s_small, 16)
                    sp.dma_start(coefc[:], consts[0:RANK, C_BATCH:C_BATCH + 9]).then_inc(s_small, 16)
                if g == PG_X0:
                    sp.wait_ge(w_acc, NB)
                    sp.wait_ge(p_w, NB)
                    sp.wait_ge(xq, NB)
                    sp.dma_start(mask8[:].rearrange("p (b k) -> p b k", b=NB),
                                 mask.rearrange("b q k -> q b k")).then_inc(s_mask, 16)
                    for p in range(2):
                        sp.dma_start(pb[p][:].rearrange("p (h k) -> p h k", h=2),
                                     posbias[2 * p:2 * p + 2].rearrange("h q k -> q h k")).then_inc(s_pb[p], 16)
                if g > PG_X0 + 1 and g - PG_X0 < PAIRS:
                    p = g - PG_X0
                    sp.wait_ge(bm_done, NB * (p - 1))
                    sp.dma_start(pb[p % 2][:].rearrange("p (h k) -> p h k", h=2),
                                 posbias[2 * p:2 * p + 2].rearrange("h q k -> q h k")).then_inc(s_pb[p % 2], 16)
            sp.wait_ge(raw_free[2], NPAGES)
            sp.dma_start(bias_b, ffn_bias.partition_broadcast(P)).then_inc(s_bias, 16)
            for b in range(NB):
                sp.wait_ge(f_o, b + 1)
                sp.dma_start(out[b], yo[b % 2]).then_inc(f_out[b % 2], 16)
            for i in range(2):
                sp.wait_ge(f_out[i], 16 * NB // 2)

        @block.tensor
        def _(pe):
            def transposes(src, dst, done):
                for e in range(EC):
                    i = nc.tensor.transpose(dst[:, e * P:(e + 1) * P], src[:, e * P:(e + 1) * P], ident[:])
                i.then_inc(done, 1)

            read_by = {"x": (x_lo, lambda a: 2 * a[0] + a[1] + 1), "q": (q_rope, lambda a: QP * a[0] + a[1] + 1),
                       "k": (k_rope, lambda a: a[0] + 1), "v": (v_evac, lambda a: a[0] + 1),
                       "s": (ks_ev, lambda a: QP * a[0] + a[1] + 1), "o": (ot_lo, lambda a: a + 1),
                       "n": (b_lo, lambda a: a + 1)}
            bank_user = []

            def take_bank(kind, a):
                if bank_user:
                    s, count = read_by[bank_user[-1][0]]
                    pe.wait_ge(s, count(bank_user[-1][1]))
                bank_user.append((kind, a))

            def chunks(H, L, e, cols):
                c = slice(e * NB * P + cols.start, e * NB * P + cols.stop)
                return H[:, c], L[:, c]

            def s_piece(kind, a):
                if kind == "w":
                    s_out(a)
                    return
                take_bank(kind, a)
                if kind == "x":
                    pe.wait_ge(xn_done, 2 * a[0] + a[1] + 1)
                    transposes(row[0], bPJ, p_x)
                if kind == "n":
                    pe.wait_ge(xq, a + 1)
                    transposes(row[0], bPJ, b_x)
                if kind == "o":
                    pe.wait_ge(o_norm, a + 1)
                    transposes(so, bPJ, p_ot)
                tokens = slice(2 * P * a[0], 2 * P * (a[0] + 1)) if kind in "qkv" else None
                if kind == "q":
                    pe.wait_ge(x_lo, 2 * a[0] + 2)
                    for i in range(2):
                        c = 2 * a[1] + i
                        for e in range(EC):
                            w = slice(e * PART + c * P, e * PART + (c + 1) * P)
                            m = split3(nc, bPJ[:, i * 2 * P:(i + 1) * 2 * P], XTH[:, w], XTL[:, w],
                                       *chunks(xTH, xTL, e, tokens), e == 0, e == EC - 1)
                    m.then_inc(p_q, 1)
                if kind == "k":
                    for i in range(2):
                        for e in range(EC):
                            w = slice(i * D + e * P, i * D + (e + 1) * P)
                            m = split3(nc, bPJ[:, i * 2 * P:(i + 1) * 2 * P], WH[1][:, w], WL[1][:, w],
                                       *chunks(xTH, xTL, e, tokens), e == 0, e == EC - 1)
                    m.then_inc(p_k, 1)
                if kind == "v":
                    for i in range(2):
                        t = slice(tokens.start + i * P, tokens.start + (i + 1) * P)
                        for e in range(EC):
                            w = slice(PART + e * P, PART + (e + 1) * P)
                            m = split3(nc, bPJ[:, i * P:(i + 1) * P], *chunks(xTH, xTL, e, t),
                                       WH[1][:, w], WL[1][:, w], e == 0, e == EC - 1)
                    m.then_inc(p_v, 1)
                if kind == "s":
                    pe.wait_ge(k_rope, a[0] + 1)
                    for i in range(2):
                        c = C_SEL + (2 * a[1] + i) * P
                        m = nc.tensor.matmul(bPJ[:, i * 2 * P:(i + 1) * 2 * P], cst[:, c:c + P], kr[0][:],
                                             start=True, stop=True)
                    m.then_inc(p_ks, 1)

            def head_cols(G, j):
                c, bb = 4 * (G // 4 % 2) + j, G // GROUPS % 2
                return c // 2, slice((c % 2) * 2 * P + bb * P, (c % 2) * 2 * P + (bb + 1) * P)

            def s_scores(G):
                pair, h = G // (2 * GROUPS), G % 4
                if G % (2 * GROUPS) in (0, 4):
                    half = QP // 2 * (G % (2 * GROUPS) // 4 + 1)
                    pe.wait_ge(q_rope, QP * pair + half)
                    pe.wait_ge(ks_ev, QP * pair + half)
                at_least(pe, v_stt, G - 3)
                r = slice(32 * h, 32 * h + 32)
                for j in range(4):
                    q, c = head_cols(G, j)
                    i = nc.tensor.matmul(bS[h][:, j * P:(j + 1) * P], qT[pair % 2][q][r, c],
                                         kS[pair % 2][q][r, c], start=True, stop=True)
                i.then_inc(p_s, 1)

            def s_probs_t(G):
                pe.wait_ge(a_exp, G + 1)
                at_least(pe, pt_ev, G)
                for j in range(4):
                    i = nc.tensor.transpose(bPT[:, j * P:(j + 1) * P], sP[G % 4][:, j * P:(j + 1) * P], ident[:])
                i.then_inc(p_t, 1)

            def s_values(G):
                b, pair = G // GROUPS, G // (2 * GROUPS)
                pe.wait_ge(pt_ev, G + 1)
                if G % GROUPS == 0:
                    pe.wait_ge(v_evac, pair + 1)
                    at_least(pe, o_norm, b)
                for j in range(4):
                    kv = 4 * (G // 4 % 2) + j
                    head = GR * kv + G % 4
                    v0 = (b % 2) * P + kv * SD
                    i = nc.tensor.matmul(bO[:, head * SD:(head + 1) * SD], sPT[G % 2][:, j * P:(j + 1) * P],
                                         vS[pair % 2][:, v0:v0 + SD], start=True, stop=True)
                i.then_inc(p_pv, 1)

            def s_out(b):
                pe.wait_ge(ot_lo, b + 1)
                at_least(pe, w_acc, b)
                for e in range(EC):
                    w = slice(2 * PART + e * D, 2 * PART + (e + 1) * D)
                    i = split3(nc, bW[:], soTH[:, e * P:(e + 1) * P], soTL[:, e * P:(e + 1) * P],
                               WH[1][:, w], WL[1][:, w], e == 0, e == EC - 1)
                i.then_inc(p_w, 1)

            pe.wait_ge(s_ident, 16)
            for name in FIRST:
                if name == "q0":
                    for i in range(4):
                        pe.wait_ge(raw_free[i], PG_SQ + 1)
                if name == "k":
                    for i in range(4):
                        pe.wait_ge(raw_free[i], PG_SKVO + 1)
                    pe.wait_ge(s_const, 16)
                s_piece(name[0], (0, int(name[1:] or 0)))
            s_scores(0)
            s_scores(1)
            for G in range(SLOTS):
                if G + 2 < SLOTS:
                    s_scores(G + 2)
                s_probs_t(G)
                if G:
                    s_values(G - 1)
                if beside(G):
                    s_piece(*beside(G))
            s_values(SLOTS - 1)

            def c_project_qk(n, q):
                k, f, slot = q % 4, (q // 4) % 2, (q // 8) % 2
                head, keys = k // 2, k % 2
                if q % 8 == 0:
                    pe.wait_ge(raw_free[0], PG_X0 + 1 + n // 8)
                if q % 8 == 1:
                    pe.wait_ge(raw_free[1], PG_X0 + 1 + n // 8)
                at_least(pe, qk_lo, n)
                XH, XL = (CTH, CTL) if keys else (XTH, XTL)
                for e in range(EC):
                    w = slice(keys * PART + e * 2 * P + head * P, keys * PART + e * 2 * P + (head + 1) * P)
                    m = slice(e * NB * P + f * HALF * P, e * NB * P + (f + 1) * HALF * P)
                    i = split3(nc, bQK[:], WH[slot][:, w], WL[slot][:, w], XH[:, m], XL[:, m],
                               e == 0, e == EC - 1)
                i.then_inc(qk_mm, 1)

            def c_project_v(n, q):
                b, slot = q % 8, (q // 8) % 2
                if q % 8 == 0:
                    pe.wait_ge(raw_free[2], PG_X0 + 1 + n // 8)
                at_least(pe, v_lo, n)
                for e in range(EC):
                    m = slice(e * NB * P + b * P, e * NB * P + (b + 1) * P)
                    w = slice(2 * PART + e * 2 * P, 2 * PART + (e + 1) * 2 * P)
                    i = split3(nc, bV[:, 0:2 * P], CTH[:, m], CTL[:, m], WH[slot][:, w], WL[slot][:, w],
                               e == 0, e == EC - 1)
                i.then_inc(v_mm, 1)

            def c_scores(t, q):
                f, k = (q // 4) % 2, q % 4
                if k == 0:
                    pe.wait_ge(qk_lo, t + HALF)
                at_least(pe, c_add, t)
                c = slice(k * P, (k + 1) * P)
                for h in range(2):
                    i = split3_wide(nc, bSC[:, h * 2 * P:(h + 1) * 2 * P], QH[f][h][:, c], QL[f][h][:, c],
                                    KHL[f][h][:, k * 2 * P:(k + 1) * 2 * P])
                i.then_inc(c_s, 1)

            def c_probs_t(t, q):
                pe.wait_ge(c_norm, t + 1)
                at_least(pe, c_tlo, t)
                for h in range(2):
                    i = nc.tensor.transpose(bT[:, h * P:(h + 1) * P], cP[q % 2][:, h * P:(h + 1) * P], ident[:])
                i.then_inc(c_t, 1)

            def c_values(t, q):
                f, k = (q // 4) % 2, q % 4
                pe.wait_ge(c_tlo, t + 1)
                pe.wait_ge(v_lo, t + 1)
                at_least(pe, c_olo, t)
                for h in range(2):
                    c, hl = slice(h * P, (h + 1) * P), slice(h * 2 * P, (h + 1) * 2 * P)
                    i = split3_wide(nc, bPV[:, hl], VH[f][k][:, c], VL[f][k][:, c], cT[:, hl])
                i.then_inc(c_pv, 1)

            def c_output(t, q):
                slot = (q // 8) % 2
                if q % 8 == 0:
                    pe.wait_ge(raw_free[3], PG_X0 + 1 + t // 8)
                pe.wait_ge(c_olo, t + 1)
                at_least(pe, c_acc, t)
                for h in range(2):
                    c, w = slice(h * P, (h + 1) * P), slice(3 * PART + h * D, 3 * PART + (h + 1) * D)
                    i = split3(nc, bOUT[:], oTH[:, c], oTL[:, c], WH[slot][:, w], WL[slot][:, w],
                               h == 0, h == 1)
                i.then_inc(c_out, 1)

            def c_step(t, q):
                c_scores(t, q)
                if not isinstance(t, int) or t >= 1:
                    c_probs_t(t - 1, (q - 1) % LOOP)
                ahead = not isinstance(t, int) or t + HALF < STEPS
                if ahead:
                    c_project_qk(t + HALF, (q + HALF) % LOOP)
                if not isinstance(t, int) or t >= 2:
                    c_output(t - 2, (q - 2) % LOOP)
                if not isinstance(t, int) or t >= 1:
                    c_values(t - 1, (q - 1) % LOOP)
                if ahead:
                    c_project_v(t + HALF, (q + HALF) % LOOP)

            def f_turn(b):
                pe.wait_ge(f_n, b + 1)
                at_least(pe, f_lo, b - 1)
                transposes(frow[b % 2], bank[6 + b % 2], f_x)

            for i in range(4):
                pe.wait_ge(raw_free[i], PG_CTX + 1)
            pe.wait_ge(b_lo, HALF)
            for n in range(HALF):
                c_project_qk(n, n)
                if TAIL_PIECES[n]:
                    s_piece(TAIL_PIECES[n], NB - 1)
                c_project_v(n, n)
            pe.wait_ge(b_lo, NB)
            for t in range(HEAD):
                c_step(t, t)
            with pe.Fori(0, ROUNDS) as r:
                for q in range(LOOP):
                    c_step(r * LOOP + (HEAD + q), (HEAD + q) % LOOP)
            for t in range(STEPS - TAIL, STEPS):
                c_step(t, t % LOOP)
                for b in F_TURN[t]:
                    f_turn(b)
            last = STEPS - 1
            c_probs_t(last, last % LOOP)
            c_output(last - 1, (last - 1) % LOOP)
            f_turn(5)
            c_values(last, last % LOOP)
            c_output(last, last % LOOP)

            def f_adapter(h):
                pe.wait_ge(f_lo, HALF * (h + 1))
                pe.wait_ge(raw_free[2], NPAGES)
                for e in range(EC):
                    m = slice(e * NB * P + h * HALF * P, e * NB * P + (h + 1) * HALF * P)
                    w = slice(2 * PART + e * RANK, 2 * PART + (e + 1) * RANK)
                    i = split3(nc, bank[h][0:RANK, :], fW[:, w], fL[:, w], XTH[:, m], XTL[:, m],
                               e == 0, e == EC - 1)
                i.then_inc(f_a, 1)
            def f_product(b):
                y = bank[2 + b % 3]
                at_least(pe, f_o, b - 2)
                for e in range(EC):
                    m = slice(e * NB * P + b * P, e * NB * P + (b + 1) * P)
                    w = slice(e * D, (e + 1) * D)
                    split3(nc, y[:], XTH[:, m], XTL[:, m], fW[:, w], fL[:, w], e == 0, False)

            def f_adapted(b):
                pe.wait_ge(f_alo, b // HALF + 1)
                c = slice(b * P, (b + 1) * P)
                split3(nc, bank[2 + b % 3][:], laH[:, c], laL[:, c], lbH, lbL, False, True).then_inc(f_y, 1)

            f_adapter(0)
            f_turn(6)
            for i in (0, 1, 3):
                pe.wait_ge(raw_free[i], NPAGES)
            f_product(0)
            f_turn(7)
            f_product(1)
            f_adapted(0)
            f_adapter(1)
            f_adapted(1)
            for b in range(2, NB):
                f_product(b)
                f_adapted(b)

        @block.scalar
        def _(act):
            def copy(dst, src):
                return nc.scalar.activation(dst, src, ACT.Copy)

            def high(g):
                H, _ = page_slot(g)
                for i in range(4):
                    act.wait_ge(s_raw[i], 16 * (g + 1))
                    copy(part(H, i), raw[i][:]).then_inc(hi_done[i], 1)

            def high_piece(t, q):
                piece = page_piece(t, q)
                if not piece:
                    return
                g, i, slot = piece
                if i == 3:
                    act.wait_ge(c_out, t - 2)
                else:
                    act.wait_ge(qk_mm, t - i + 4)
                    act.wait_ge(v_mm, t - i + 4)
                act.wait_ge(s_raw[i], 16 * (g + 1))
                copy(part(WH[slot], i), raw[i][:]).then_inc(hi_done[i], 1)

            def rows_hi(dst, b, src):
                return copy(dst[:].rearrange("p (e t) -> p e t", e=EC)[:, :, b * P:(b + 1) * P],
                            src[:].rearrange("p (e t) -> p e t", e=EC))

            def s_exp(G):
                act.wait_ge(v_max, G + 1)
                for j in range(4):
                    head = GR * (4 * (G // 4 % 2) + j) + G % 4
                    c = sP[G % 4][:, j * P:(j + 1) * P]
                    i = nc.scalar.activation(c, c, ACT.Exp, bias=smax[G % 4][:, j:j + 1],
                                             accum_out=ssum[G // GROUPS % 2][:, head:head + 1])
                i.then_inc(a_exp, 1)

            def s_piece(kind, a):
                if kind == "x":
                    b = 2 * a[0] + a[1]
                    act.wait_ge(p_x, b + 1)
                    rows_hi(xTH, b, bPJ).then_inc(x_hi, 1)
                if kind == "n":
                    act.wait_ge(b_x, a + 1)
                    rows_hi(XTH, a, bPJ).then_inc(b_hi, 1)
                if kind == "o":
                    act.wait_ge(p_ot, a + 1)
                    copy(soTH, bPJ[:]).then_inc(ot_hi, 1)
                if kind == "v":
                    act.wait_ge(p_v, a[0] + 1)
                    copy(vS[a[0] % 2][:], bPJ[:, 0:2 * P]).then_inc(v_evac, 1)
                if kind == "s":
                    act.wait_ge(p_ks, QP * a[0] + a[1] + 1)
                    copy(kS[a[0] % 2][a[1]][:], bPJ[:]).then_inc(ks_ev, 1)

            for name in FIRST:
                if name == "q0":
                    high(PG_SQ)
                    high(PG_SKVO)
                s_piece(name[0], (0, int(name[1:] or 0)))
            s_exp(0)
            for G in range(SLOTS):
                if G + 1 < SLOTS:
                    s_exp(G + 1)
                if G == SLOTS - 2 * GROUPS:
                    act.wait_ge(p_v, NB // 2)
                    high(PG_CTX)
                if G == SLOTS - GROUPS:
                    high(PG_X0)
                if beside(G):
                    s_piece(*beside(G))

            def c_qk_hi(n, q):
                k, f = q % 4, (q // 4) % 2
                act.wait_ge(qk_mm, n + 1)
                if k % 2:
                    copy(halves(KHL[f][k // 2][:], 0), blocks(bQK[:])).then_inc(qk_hi, 1)
                else:
                    copy(QH[f][k // 2][:], bQK[:]).then_inc(qk_hi, 1)

            def c_v_hi(n, q):
                act.wait_ge(v_mm, n + 1)
                copy(VH[(q // 4) % 2][q % 4][:], bV[:, 0:2 * P]).then_inc(v_hi, 1)

            def c_t_hi(t, q):
                act.wait_ge(c_t, t + 1)
                at_least(act, c_pv, t)
                copy(halves(cT[:], 0), blocks(bT[:, 0:2 * P])).then_inc(c_thi, 1)

            def c_exps(t, q):
                act.wait_ge(c_max, t + 1)
                for h in range(2):
                    c = cP[q % 2][:, h * P:(h + 1) * P]
                    i = nc.scalar.activation(c, c, ACT.Exp, bias=cmax[q % 2][:, h:h + 1],
                                             accum_out=csum[q % 2][:, h:h + 1])
                i.then_inc(c_exp, 1)

            def c_o_hi(t, q):
                act.wait_ge(c_pv, t + 1)
                at_least(act, c_out, t)
                copy(blocks(oTH[:]), halves(bPV[:], 0)).then_inc(c_ohi, 1)

            def c_step(t, q):
                if not isinstance(t, int) or t >= 1:
                    c_t_hi(t - 1, (q - 1) % LOOP)
                c_exps(t, q)
                ahead = not isinstance(t, int) or t + HALF < STEPS
                if ahead:
                    c_qk_hi(t + HALF, (q + HALF) % LOOP)
                if not isinstance(t, int) or t >= 1:
                    c_o_hi(t - 1, (q - 1) % LOOP)
                if ahead:
                    c_v_hi(t + HALF, (q + HALF) % LOOP)
                high_piece(t, q)

            def f_hi_rows(b):
                act.wait_ge(f_x, b + 1)
                rows_hi(XTH, b, bank[6 + b % 2]).then_inc(f_hi, 1)

            for n in range(HALF):
                c_qk_hi(n, n)
                if TAIL_PIECES[n]:
                    s_piece(TAIL_PIECES[n], NB - 1)
                c_v_hi(n, n)
            act.wait_ge(xq, NB)
            act.wait_ge(w_acc, NB)
            high(PG_X0 + 1)
            for t in range(HEAD):
                c_step(t, t)
            with act.Fori(0, ROUNDS) as r:
                for q in range(LOOP):
                    c_step(r * LOOP + (HEAD + q), (HEAD + q) % LOOP)
            for t in range(STEPS - TAIL, STEPS):
                c_step(t, t % LOOP)
                for b in F_TURN[t]:
                    f_hi_rows(b)
            c_t_hi(STEPS - 1, (STEPS - 1) % LOOP)
            f_hi_rows(5)
            c_o_hi(STEPS - 1, (STEPS - 1) % LOOP)

            for h in range(2):
                f_hi_rows(6 + h)
                act.wait_ge(f_am, h + 1)
                c = slice(h * D, (h + 1) * D)
                copy(laH[:, c], la[:, c]).then_inc(f_ahi, 1)

        @block.vector
        def _(dve):
            v = nc.vector

            def moments(k, b):
                m, ve = (mv, mv2, mv3)[k], (veps, veps2, veps3)[k]
                v.bn_stats(st6[:, 6 * b:6 * b + 6], acc[:, b * D:(b + 1) * D]).then_inc(st_done, 1)
                dve.wait_ge(st_done, NB * k + b + 1)
                v.bn_aggr(m[:, 2 * b:2 * b + 2], st6[:, 6 * b:6 * b + 6]).then_inc(mv_done, 1)
                dve.wait_ge(mv_done, NB * k + b + 1)
                v.tensor_scalar(ve[:, b:b + 1], m[:, 2 * b + 1:2 * b + 2], EPS, None, ALU.add)\
                 .then_inc(ve_done, 1)

            def normalise(dst, k, b):
                m, r = (mv, mv2, mv3)[k], (rstd, rstd2, rstd3)[k]
                dve.wait_ge(rstd_done, NB * k + b + 1)
                return v.tensor_scalar(dst, acc[:, b * D:(b + 1) * D], m[:, 2 * b:2 * b + 1], r[:, b:b + 1],
                                       ALU.subtract, ALU.mult)

            def rows_lo(L, H, b, src):
                c, h = (t.rearrange("p (e t) -> p e t", e=EC)[:, :, b * P:(b + 1) * P]
                        for t in (L[:], H[:].bitcast(F32)))
                return v.tensor_tensor(c, src[:].rearrange("p (e t) -> p e t", e=EC), h, ALU.subtract)

            def low(g, parts=range(4)):
                H, L = page_slot(g)
                for i in parts:
                    dve.wait_ge(hi_done[i], g + 1)
                    v.tensor_tensor(part(L, i), raw[i][:], part(H, i).bitcast(F32), ALU.subtract)\
                     .then_inc(raw_free[i], 1)

            def s_before(kind, a):
                if kind == "x":
                    b = 2 * a[0] + a[1]
                    at_least(dve, p_x, b)
                    normalise(row[0][:], 0, b).then_inc(xn_done, 1)
                if kind == "n":
                    if a == 0:
                        dve.wait_ge(p_x, NB)
                        dve.wait_ge(s_lnw, 16)
                    at_least(dve, b_x, a)
                    normalise(row[0][:], 1, a).then_inc(hid, 1)
                    dve.wait_ge(hid, a + 1)
                    c = acc[:, a * D:(a + 1) * D]
                    v.tensor_tensor(c, c, row[0][:], ALU.add).then_inc(hadd, 1)
                    dve.wait_ge(rms_ready, a + 1)
                    dve.wait_ge(hadd, a + 1)
                    v.scalar_tensor_tensor(out=row[0][:], in0=row[0][:], scalar=rms[:, a:a + 1],
                                           in1=lnw_b[:], op0=ALU.mult, op1=ALU.mult).then_inc(xq, 1)

            def s_piece(kind, a):
                if kind == "x":
                    b = 2 * a[0] + a[1]
                    dve.wait_ge(x_hi, b + 1)
                    rows_lo(xTL, xTH, b, bPJ).then_inc(x_lo, 1)
                if kind == "n":
                    dve.wait_ge(b_hi, a + 1)
                    rows_lo(XTL, XTH, a, bPJ).then_inc(b_lo, 1)
                if kind == "q":
                    dve.wait_ge(p_q, QP * a[0] + a[1] + 1)
                    v.tensor_tensor(qT[a[0] % 2][a[1]][:].rearrange("p (c t) -> p c t", c=4),
                                    bPJ[:].rearrange("p (c t) -> p c t", c=4), bcast(tabq, 4),
                                    ALU.mult).then_inc(q_rope, 1)
                if kind == "k":
                    dve.wait_ge(p_k, a[0] + 1)
                    at_least(dve, p_ks, QP * a[0])
                    for i, table in enumerate((cosk, sink)):
                        v.tensor_tensor(kr[i][:].rearrange("p (b t) -> p b t", b=2),
                                        bPJ[:, i * 2 * P:(i + 1) * 2 * P].rearrange("p (b t) -> p b t", b=2),
                                        bcast(table, 2), ALU.mult).then_inc(k_part, 1)
                    dve.wait_ge(k_part, 2 * a[0] + 2)
                    v.tensor_tensor(kr[0][:], kr[0][:], kr[1][:], ALU.add).then_inc(k_rope, 1)
                if kind == "o":
                    dve.wait_ge(ot_hi, a + 1)
                    v.tensor_tensor(soTL, bPJ[:], soTH.bitcast(F32), ALU.subtract).then_inc(ot_lo, 1)
                if kind == "w":
                    dve.wait_ge(p_w, a + 1)
                    c = acc[:, a * D:(a + 1) * D]
                    v.tensor_tensor(c, bW[:], c, ALU.add).then_inc(w_acc, 1)
                    dve.wait_ge(w_acc, a + 1)
                    moments(1, a)

            def s_mask_max(G):
                dve.wait_ge(p_s, G + 1)
                at_least(dve, p_t, G - 3)
                v.scalar_tensor_tensor(out=sP[G % 4][:].rearrange("p (c t) -> p c t", c=4),
                                       in0=bS[G % 4][:].rearrange("p (c t) -> p c t", c=4), scalar=SSCALE,
                                       in1=bcast(causal, 4), op0=ALU.mult, op1=ALU.add).then_inc(v_stt, 1)
                dve.wait_ge(v_stt, G + 1)
                v.tensor_reduce(smax[G % 4][:], sP[G % 4][:].rearrange("p (c t) -> p c t", c=4), AX.X,
                                ALU.max, negate=True).then_inc(v_max, 1)

            def s_probs_evac(G):
                dve.wait_ge(p_t, G + 1)
                at_least(dve, p_pv, G - 1)
                v.tensor_copy(sPT[G % 2][:], bPT[:]).then_inc(pt_ev, 1)

            def s_o_norm(b):
                dve.wait_ge(a_exp, GROUPS * (b + 1))
                v.reciprocal(srec[:], ssum[b % 2][:]).then_inc(o_rec, 1)
                dve.wait_ge(o_rec, b + 1)
                dve.wait_ge(p_pv, GROUPS * (b + 1))
                at_least(dve, p_ot, b)
                v.tensor_tensor(so[:].rearrange("p (h d) -> p h d", d=SD),
                                bO[:].rearrange("p (h d) -> p h d", d=SD),
                                srec[:].unsqueeze(2).to_broadcast([P, SH, SD]), ALU.mult).then_inc(o_norm, 1)

            for b in range(2):
                dve.wait_ge(s_x[b], 16)
                moments(0, b)
            for name in FIRST:
                piece = name[0], (0, int(name[1:] or 0))
                if name == "q0":
                    low(PG_SQ)
                    dve.wait_ge(s_const, 16)
                s_before(*piece)
                s_piece(*piece)
                if name[0] == "q":
                    low(PG_SKVO, [int(name[1])])
            for b in range(2, NB):
                dve.wait_ge(s_x[b], 16)
                moments(0, b)
            s_mask_max(0)
            s_mask_max(1)
            for G in range(SLOTS):
                if beside(G):
                    s_before(*beside(G))
                if G + 2 < SLOTS:
                    s_mask_max(G + 2)
                s_probs_evac(G)
                if G % GROUPS == 0 and G:
                    s_o_norm(G // GROUPS - 1)
                if beside(G):
                    s_piece(*beside(G))
            s_o_norm(NB - 1)

            def c_qk_lo(n, q):
                k, f = q % 4, (q // 4) % 2
                dve.wait_ge(qk_hi, n + 1)
                if k % 2:
                    KK = KHL[f][k // 2][:]
                    v.tensor_tensor(halves(KK, 1), blocks(bQK[:]), halves(KK.bitcast(F32), 0), ALU.subtract)\
                     .then_inc(qk_lo, 1)
                else:
                    v.tensor_tensor(QL[f][k // 2][:], bQK[:], QH[f][k // 2][:].bitcast(F32), ALU.subtract)\
                     .then_inc(qk_lo, 1)

            def c_v_lo(n, q):
                f, k = (q // 4) % 2, q % 4
                dve.wait_ge(v_hi, n + 1)
                v.tensor_tensor(VL[f][k][:], bV[:, 0:2 * P], VH[f][k][:].bitcast(F32), ALU.subtract)\
                 .then_inc(v_lo, 1)

            def c_add_max(t, q):
                dve.wait_ge(c_s, t + 1)
                dve.wait_ge(bm_done, t + 1)
                at_least(dve, c_t, t - 1)
                v.tensor_tensor(blocks(cP[q % 2]), halves(bSC[:], 0), blocks(bm[q % 2]), ALU.add)\
                 .then_inc(c_half, 1)
                dve.wait_ge(c_half, t + 1)
                v.tensor_tensor(blocks(cP[q % 2]), halves(bSC[:], 1), blocks(cP[q % 2]), ALU.add)\
                 .then_inc(c_add, 1)
                dve.wait_ge(c_add, t + 1)
                v.tensor_reduce(cmax[q % 2][:], cP[q % 2].rearrange("p (h k) -> p h k", h=2), AX.X,
                                ALU.max, negate=True).then_inc(c_max, 1)

            def c_t_lo(t, q):
                dve.wait_ge(c_thi, t + 1)
                v.tensor_tensor(halves(cT[:], 1), blocks(bT[:, 0:2 * P]), halves(cT[:].bitcast(F32), 0),
                                ALU.subtract).then_inc(c_tlo, 1)

            def c_normalise(t, q):
                b = q % NB
                dve.wait_ge(c_exp, t + 1)
                v.reciprocal(crec[q % 2][:], csum[q % 2][:]).then_inc(c_rec, 1)
                dve.wait_ge(c_rec, t + 1)
                for h in range(2):
                    c = cP[q % 2][:, h * P:(h + 1) * P]
                    i = v.tensor_scalar(c, c, crec[q % 2][:, h:h + 1], valid[:, b:b + 1], ALU.mult, ALU.mult)
                i.then_inc(c_norm, 1)

            def c_accumulate(t, q):
                b = q % NB
                dve.wait_ge(c_out, t + 1)
                at_least(dve, c_acc, t - NB + 1)
                a = acc[:, b * D:(b + 1) * D]
                v.tensor_tensor(a, bOUT[:], a, ALU.add).then_inc(c_acc, 1)


            def c_o_lo(t, q):
                dve.wait_ge(c_ohi, t + 1)
                v.tensor_tensor(blocks(oD[:]), halves(bPV[:], 0), blocks(oTH[:].bitcast(F32)), ALU.subtract)\
                 .then_inc(c_odiff, 1)
                dve.wait_ge(c_odiff, t + 1)
                v.tensor_tensor(blocks(oTL[:]), halves(bPV[:], 1), blocks(oD[:]), ALU.add).then_inc(c_olo, 1)

            def c_step(t, q):
                c_add_max(t, q)
                if not isinstance(t, int) or t >= 1:
                    c_t_lo(t - 1, (q - 1) % LOOP)
                c_normalise(t, q)
                ahead = not isinstance(t, int) or t + HALF < STEPS
                if ahead:
                    c_qk_lo(t + HALF, (q + HALF) % LOOP)
                if not isinstance(t, int) or t >= 2:
                    c_accumulate(t - 2, (q - 2) % LOOP)
                if not isinstance(t, int) or t >= 1:
                    c_o_lo(t - 1, (q - 1) % LOOP)
                if ahead:
                    c_v_lo(t + HALF, (q + HALF) % LOOP)

            def f_norm(b):
                dve.wait_ge(raw_free[b % 2], NPAGES)
                at_least(dve, f_x, b - 1)
                normalise(frow[b % 2], 2, b).then_inc(f_n, 1)

            def f_lo_rows(b):
                dve.wait_ge(f_hi, b + 1)
                rows_lo(XTL, XTH, b, bank[6 + b % 2]).then_inc(f_lo, 1)

            for n in range(HALF):
                if TAIL_PIECES[n] == "n":
                    s_before("n", NB - 1)
                c_qk_lo(n, n)
                if TAIL_PIECES[n]:
                    s_piece(TAIL_PIECES[n], NB - 1)
                c_v_lo(n, n)

            dve.wait_ge(s_small, 32)
            v.tensor_copy(st_f[:], st_i[:]).then_inc(co, 1)
            dve.wait_ge(co, 1)
            for i in range(4):
                v.tensor_scalar(cnt[:, i * NB:(i + 1) * NB], coefc[:, 0:NB], st_f[:, i:i + 1], None, ALU.is_ge)\
                 .then_inc(co, 1)
            dve.wait_ge(co, 5)
            v.tensor_reduce(cnt[:, 4 * NB:5 * NB], cnt[:, 0:4 * NB].rearrange("p (i b) -> p b i", i=4), AX.X,
                            ALU.add).then_inc(co, 1)
            dve.wait_ge(co, 6)
            v.tensor_scalar(coef[:], cnt[:, 4 * NB:5 * NB], coefc[:, NB:NB + 1], None, ALU.is_equal)\
             .then_inc(co_done, 1)
            dve.wait_ge(s_mask, 16)
            dve.wait_ge(hadd, NB)
            v.tensor_reduce(valid[:], mask8[:].rearrange("p (b k) -> p b k", b=NB), AX.X, ALU.max)\
             .then_inc(valid_done, 1)
            v.tensor_scalar(madd[:], mask8[:], 1.0, -MASKED, ALU.subtract, ALU.mult).then_inc(madd_done, 1)
            dve.wait_ge(valid_done, 1)

            for t in range(HEAD):
                c_step(t, t)
            with dve.Fori(0, ROUNDS) as r:
                for q in range(LOOP):
                    c_step(r * LOOP + (HEAD + q), (HEAD + q) % LOOP)
            for t in range(STEPS - TAIL, STEPS):
                for b in F_TURN[t]:
                    f_norm(b)
                c_step(t, t % LOOP)
                for b in F_STAT[t]:
                    dve.wait_ge(c_acc, STEPS - NB + b + 1)
                    moments(2, b)
                for b in F_TURN[t]:
                    f_lo_rows(b)
            last = STEPS - 1
            c_t_lo(last, last % LOOP)
            f_norm(5)
            c_accumulate(last - 1, (last - 1) % LOOP)
            dve.wait_ge(c_acc, STEPS - 1)
            moments(2, NB - 2)
            f_lo_rows(5)
            f_norm(NB - 2)
            c_o_lo(last, last % LOOP)
            c_accumulate(last, last % LOOP)
            dve.wait_ge(c_acc, STEPS)
            moments(2, NB - 1)
            f_lo_rows(NB - 2)

            def f_adapter(h):
                dve.wait_ge(f_a, h + 1)
                for b in range(h * HALF, (h + 1) * HALF):
                    i = v.tensor_scalar(la[:, b * P:(b + 1) * P], bank[h][0:RANK, (b % HALF) * P:(b % HALF + 1) * P],
                                        coef[:, b:b + 1], None, ALU.mult)
                i.then_inc(f_am, 1)
                c = slice(h * D, (h + 1) * D)
                dve.wait_ge(f_ahi, h + 1)
                v.tensor_tensor(laL[:, c], la[:, c], laH[:, c].bitcast(F32), ALU.subtract).then_inc(f_alo, 1)

            def f_sum(b):
                dve.wait_ge(f_y, b + 1)
                dve.wait_ge(f_bias, b + 1)
                at_least(dve, f_out[b % 2], 16 * (b // 2))
                v.tensor_tensor(yo[b % 2], bank[2 + b % 3][:], acc[:, b * D:(b + 1) * D], ALU.add)\
                 .then_inc(f_o, 1)

            dve.wait_ge(raw_free[3], NPAGES)
            dve.wait_ge(co_done, 1)
            f_norm(NB - 1)
            f_adapter(0)
            f_lo_rows(NB - 1)
            f_sum(0)
            f_adapter(1)
            for b in range(1, NB):
                f_sum(b)

        @block.gpsimd
        def _(pool):
            g_ = nc.gpsimd

            def low(g, i, slot=None):
                H, L = (WH[slot], WL[slot]) if slot is not None else page_slot(g)
                pool.wait_ge(hi_done[i], g + 1)
                g_.tensor_tensor(part(L, i), raw[i][:], part(H, i).bitcast(F32), ALU.subtract)\
                  .then_inc(raw_free[i], 1)

            def rsqrt(k, b):
                ve, r = (veps, veps2, veps3)[k], (rstd, rstd2, rstd3)[k]
                pool.wait_ge(ve_done, NB * k + b + 1)
                g_.tensor_tensor(r[:, b:b + 1], ve[:, b:b + 1], mhalf[:], ALU.pow).then_inc(rstd_done, 1)

            def rms_factor(b):
                r, m = rstd2[:, b:b + 1], rms[:, b:b + 1]
                pool.wait_ge(rstd_done, NB + b + 1)
                g_.tensor_tensor(m, r, r, ALU.mult).then_inc(ms_step, 1)
                pool.wait_ge(ms_step, 3 * b + 1)
                g_.tensor_tensor(m, m, mv2[:, 2 * b + 1:2 * b + 2], ALU.mult).then_inc(ms_step, 1)
                pool.wait_ge(ms_step, 3 * b + 2)
                g_.tensor_scalar(m, m, EPS, None, ALU.add).then_inc(ms_step, 1)
                pool.wait_ge(ms_step, 3 * b + 3)
                g_.tensor_tensor(m, m, mhalf[:], ALU.pow).then_inc(rms_ready, 1)

            g_.memset(mhalf[:], -0.5).then_inc(half_set, 1)
            pool.wait_ge(half_set, 1)
            for b in range(NB):
                rsqrt(0, b)
            for b in range(NB):
                if b == NB - 2:
                    for i in range(4):
                        low(PG_CTX, i)
                if b == NB - 1:
                    for i in range(4):
                        low(PG_X0, i)
                rsqrt(1, b)
                rms_factor(b)

            def bias_mask(t, q):
                p, b = (q // NB) % 2, q % NB
                if b == 0:
                    pool.wait_ge(s_pb[p], 16 * (t // LOOP + 1))
                at_least(pool, c_add, t - 1)
                g_.tensor_tensor(bm[q % 2].rearrange("p (h k) -> p h k", h=2),
                                 pb[p][:].rearrange("p (h k) -> p h k", h=2),
                                 bcast(madd[:, b * P:(b + 1) * P], 2), ALU.add).then_inc(bm_done, 1)

            def c_step(t, q):
                if not isinstance(t, int) or t + 1 < STEPS:
                    bias_mask(t + 1, (q + 1) % LOOP)
                piece = page_piece(t, q)
                if piece:
                    low(*piece)

            pool.wait_ge(madd_done, 1)
            pool.wait_ge(b_x, NB)
            pool.wait_ge(p_w, NB)
            bias_mask(0, 0)
            for i in range(4):
                low(PG_X0 + 1, i)
            for t in range(HEAD):
                c_step(t, t)
            with pool.Fori(0, ROUNDS) as r:
                for q in range(LOOP):
                    c_step(r * LOOP + (HEAD + q), (HEAD + q) % LOOP)
            for t in range(STEPS - TAIL, STEPS):
                c_step(t, t % LOOP)
                for b in F_STAT[t]:
                    rsqrt(2, b)

            rsqrt(2, NB - 2)
            rsqrt(2, NB - 1)
            pool.wait_ge(s_bias, 16)
            for b in range(NB):
                a = acc[:, b * D:(b + 1) * D]
                pool.wait_ge(f_n, b + 1)
                g_.tensor_tensor(a, a, bias_b, ALU.add).then_inc(f_bias, 1)


def rope_tables(n):
    import numpy as np
    f = np.float32
    inv = (f(1.0) / f(500000.0) ** (np.arange(0, SD, 2, dtype=f) / f(SD))).astype(f)
    wavelen = (f(2.0 * np.pi) / inv).astype(f)
    low, high = 1024 / 4.0, 1024 / 1.0
    scaled = np.where(wavelen > high, inv / f(32.0), inv).astype(f)
    smooth = ((f(1024) / wavelen - f(1.0)) / f(3.0)).astype(f)
    smoothed = ((f(1.0) - smooth) * scaled / f(32.0) + smooth * scaled).astype(f)
    medium = ~(wavelen < high) & ~(wavelen > low)
    scaled = np.where(medium, smoothed, scaled).astype(f)
    freqs = np.arange(n, dtype=f)[:, None] * scaled[None, :]
    emb = np.concatenate([freqs, freqs], axis=-1).astype(f)
    return np.cos(emb).astype(f), np.sin(emb).astype(f)


def shape_constants():
    import numpy as np
    c = np.zeros((P, NCONST), np.float32)
    cos, sin = rope_tables(P)
    sign = np.where(np.arange(SD) < SD // 2, -1.0, 1.0).astype(np.float32)
    rot = (sin * sign).T
    c[:, C_TABQ:C_TABQ + P] = np.tile(np.concatenate([cos.T, rot]), (4, 1))
    c[:, C_COSK:C_COSK + P] = np.tile(cos.T, (SKV, 1))
    c[:, C_SINK:C_SINK + P] = np.tile(rot, (SKV, 1))
    for kv in range(SKV):
        for r in range(P):
            c[kv * SD + r % SD, C_SEL + kv * P + r] = 1.0
    c[:, C_CAUSAL:C_CAUSAL + P] = np.where(np.tril(np.ones((P, P), bool)), 0.0, MASKED)
    c[:, C_IDENT:C_IDENT + P] = np.eye(P)
    c[:, C_BATCH:C_BATCH + NB] = np.arange(NB)[None, :]
    c[:RANK, C_ROWS] = 2 + np.arange(RANK) // 16
    return c


def weight_pages(ctx, Wq, Wk, Wv, Wo, w_q, w_k, w_v, w_out, ffn, lora_a, lora_b):
    import numpy as np

    def on_partitions(wT):
        return wT.reshape(EC, P, -1).transpose(1, 0, 2)

    pages = np.zeros((NPAGES, 4, P, PART), np.float32)
    swapped = (np.arange(SD) + SD // 2) % SD
    rows = np.concatenate([h * SD + np.concatenate([np.arange(SD), swapped]) for h in range(SH)])
    pages[PG_SQ] = on_partitions(Wq[rows].T).transpose(1, 0, 2)
    krows = np.concatenate([h * SD + swapped for h in range(SKV)])
    pages[PG_SKVO, 0, :, :512] = on_partitions(Wk.T).reshape(P, -1)
    pages[PG_SKVO, 0, :, 512:] = on_partitions(Wk[krows].T).reshape(P, -1)
    pages[PG_SKVO, 1, :, :512] = on_partitions(Wv.T).reshape(P, -1)
    pages[PG_SKVO, 2:4] = on_partitions(Wo.T).reshape(P, 2, PART).transpose(1, 0, 2)
    pages[PG_CTX] = on_partitions(ctx.reshape(NB * P, D).T).transpose(1, 0, 2)
    for p in range(PAIRS):
        r = slice(2 * P * p, 2 * P * (p + 1))
        for i, w in enumerate((w_q, w_k, w_v)):
            pages[PG_X0 + p, i] = on_partitions(w[r].T).reshape(P, PART)
        pages[PG_X0 + p, 3] = w_out[:, r].T.reshape(2, P, D).transpose(1, 0, 2).reshape(P, PART)
    pages[PG_FFN, 0:2] = on_partitions(ffn.T).reshape(P, 2, PART).transpose(1, 0, 2)
    pages[PG_FFN, 2, :, :EC * RANK] = on_partitions(lora_a.reshape(RANK, D).T).reshape(P, -1)
    pages[PG_FFN, 3, :RANK, :D] = lora_b.transpose(0, 2, 1).reshape(RANK, D)
    return pages


def kernel(**inputs):
    import numpy as np
    import concourse.bacc as bacc
    from concourse.bass_utils import run_bass_kernel_spmd as run

    a = {k: np.asarray(v) for k, v in inputs.items()}
    arrays = {
        "x": a["x"],
        "pages": weight_pages(a["ctx_4096"], a["L0_attn_Wq"], a["L0_attn_Wk"], a["L0_attn_Wv"], a["L0_attn_Wo"],
                              a["L0_xattn_w_q"], a["L0_xattn_w_k"], a["L0_xattn_w_v"], a["L0_xattn_w_out"],
                              a["L0_ffn_weight"], a["L0_ffn_lora_A"], a["L0_ffn_lora_B"]),
        "mask": a["mask_BxSxS2_bk0"],
        "posbias": a["L0_xattn_position_bias"],
        "lnw": a["L0_xattn_ln_weight"],
        "ffn_bias": a["L0_ffn_bias"],
        "starts": a["L0_ffn_lora_start_indices"],
        "consts": shape_constants(),
    }
    nc = bacc.Bacc("TRN2", target_bir_lowering=False, num_devices=1,
                   dynamic_dma_scratch_size=1024)
    arrays = {f"in_{k}": np.ascontiguousarray(v) for k, v in arrays.items()}
    args = [nc.dram_tensor(k, v.shape, mybir.dt.from_np(v.dtype), kind="ExternalInput").ap()
            for k, v in arrays.items()]
    out = nc.dram_tensor("out", (NB, P, D), F32, kind="ExternalOutput").ap()
    build(nc, *args, out)
    r = run(nc, [arrays], core_ids=[0])
    return r.results[0]["out"]
```
